# Optimizing a Trainium2 kernel written in Bass

```python
import numpy as np
import jax
import jax.numpy as jnp

def _softmax(x, axis=-1):
    return jax.nn.softmax(x, axis=axis)

def _gelu(x):
    return jax.nn.gelu(x, approximate=True)

def _silu(x):
    return jax.nn.silu(x)

def _sigmoid(x):
    return jax.nn.sigmoid(x)

def _layernorm(x, axis=-1, eps=1e-05):
    m = jnp.mean(x, axis=axis, keepdims=True)
    v = jnp.var(x, axis=axis, keepdims=True)
    return (x - m) / jnp.sqrt(v + eps)

def _scatter_add(tgt, idx, src, axis=0):
    return tgt.at[idx].add(src)

def _segment_sum(src, seg, n):
    return jax.ops.segment_sum(src, seg, n)
kernel_name = 'mk_gnn_resnorm_d2_gnn_r8_6a01b8'

def setup_inputs(seed: int=0):
    np.random.seed(seed)
    _w = jnp.asarray

    def _rec_inputs():
        import jax
        import jax.numpy as jnp
        _gk = jax.random.key(seed)
        x = -0.0002928 + 1 * jax.random.normal(jax.random.fold_in(_gk, 1), (12500, 64), jnp.float32)
        src = jax.random.randint(jax.random.fold_in(_gk, 2), (400000,), 0, 12500, jnp.int32)
        dst = jnp.minimum((12500 * jax.random.uniform(jax.random.fold_in(_gk, 3), (400000,)) ** 2.0).astype(jnp.int32), 99999)
        _o = jnp.argsort(dst, stable=True)
        src = src[_o]
        dst = dst[_o]
        edge_attr_32 = 0.000196303 + 1.00016 * jax.random.normal(jax.random.fold_in(_gk, 12), (400000, 32), jnp.float32)
        return (x, src, dst, edge_attr_32)
    x, src, dst, edge_attr_32 = _rec_inputs()

    def _L0_gnn_setup():
        import jax, jax.numpy as jnp
        import numpy as np
        N_NODES = 8192
        N_EDGES = 131072
        IN_DIM = 64
        OUT_DIM = 64
        key = jax.random.key(seed)
        k_h, k_src, k_dst, k_fc, k_att = jax.random.split(key, 5)
        h = jax.random.normal(k_h, (N_NODES, IN_DIM), dtype=jnp.float32)
        src_r = jax.random.randint(k_src, (N_EDGES - N_NODES,), 0, N_NODES)
        dst_r = jax.random.randint(k_dst, (N_EDGES - N_NODES,), 0, N_NODES)
        loops = jnp.arange(N_NODES)
        src = jnp.concatenate([src_r, loops]).astype(jnp.int32)
        dst = jnp.concatenate([dst_r, loops]).astype(jnp.int32)
        fc_w = jax.random.normal(k_fc, (OUT_DIM, IN_DIM), dtype=jnp.float32) * (2.0 / np.sqrt(IN_DIM + OUT_DIM))
        attn_w = jax.random.normal(k_att, (1, 2 * OUT_DIM), dtype=jnp.float32) * (2.0 / np.sqrt(2 * OUT_DIM + 1))
        return {'h': h, 'fc_w': fc_w, 'attn_w': attn_w, 'src': src, 'dst': dst}
    _L0_gnn_all = _L0_gnn_setup()
    _L0_gnn_in = {k: v for k, v in _L0_gnn_all.items() if k in ('fc_w', 'attn_w')}
    del _L0_gnn_all

    def _L1_gnn_setup():
        import jax, jax.numpy as jnp
        import numpy as np
        N_NODES = 6250
        N_EDGES = 100000
        IN_DIM = 64
        EDGE_DIM = 32
        OUT_DIM = 64
        key = jax.random.key(seed)
        ks = jax.random.split(key, 7)
        x = jax.random.normal(ks[0], (N_NODES, IN_DIM), dtype=jnp.float32)
        edge_index = jax.random.randint(ks[1], (2, N_EDGES), 0, N_NODES, dtype=jnp.int64)
        edge_attr = jax.random.normal(ks[2], (N_EDGES, EDGE_DIM), dtype=jnp.float32)
        scale_msg = 1.0 / np.sqrt(IN_DIM + EDGE_DIM)
        scale_self = 1.0 / np.sqrt(IN_DIM)
        msg_w = jax.random.normal(ks[3], (IN_DIM + EDGE_DIM, OUT_DIM), dtype=jnp.float32) * scale_msg
        msg_b = jax.random.normal(ks[4], (OUT_DIM,), dtype=jnp.float32) * scale_msg
        self_w = jax.random.normal(ks[5], (IN_DIM, OUT_DIM), dtype=jnp.float32) * scale_self
        self_b = jax.random.normal(ks[6], (OUT_DIM,), dtype=jnp.float32) * scale_self
        return {'x': x, 'edge_index': edge_index, 'edge_attr': edge_attr, 'msg_w': msg_w, 'msg_b': msg_b, 'self_w': self_w, 'self_b': self_b}
    _L1_gnn_all = _L1_gnn_setup()
    _L1_gnn_in = {k: v for k, v in _L1_gnn_all.items() if k in ('msg_w', 'msg_b', 'self_w', 'self_b')}
    del _L1_gnn_all
    return {'x': x, 'src': src, 'dst': dst, 'edge_attr_32': edge_attr_32, 'L0_gnn_fc_w': _L0_gnn_in['fc_w'], 'L0_gnn_attn_w': _L0_gnn_in['attn_w'], 'L1_gnn_msg_w': _L1_gnn_in['msg_w'], 'L1_gnn_msg_b': _L1_gnn_in['msg_b'], 'L1_gnn_self_w': _L1_gnn_in['self_w'], 'L1_gnn_self_b': _L1_gnn_in['self_b']}

def reference(x, src, dst, edge_attr_32, L0_gnn_fc_w, L0_gnn_attn_w, L1_gnn_msg_w, L1_gnn_msg_b, L1_gnn_self_w, L1_gnn_self_b):
    import jax
    import jax.numpy as jnp

    def _L0_gnn_ref(h, fc_w, attn_w, src, dst):
        import jax, jax.numpy as jnp
        import numpy as np
        N_NODES = 8192
        N_EDGES = 131072
        IN_DIM = 64
        OUT_DIM = 64
        'GAT_Layer.forward (dropout=0): z = fc(h); per-edge e = leaky_relu(attn([z_src||z_dst]));\n            softmax over incoming edges of each dst node; h_out = sum alpha * z_src.'
        n = h.shape[0]
        z = h @ fc_w.T
        a_src = attn_w[0, :OUT_DIM]
        a_dst = attn_w[0, OUT_DIM:]
        es = z @ a_src
        ed = z @ a_dst
        e = jax.nn.leaky_relu(es[src] + ed[dst], negative_slope=0.01)
        emax = jnp.full((n,), -jnp.inf, dtype=e.dtype).at[dst].max(e)
        emax = jnp.where(jnp.isfinite(emax), emax, 0.0)
        w = jnp.exp(e - emax[dst])
        denom = jnp.zeros((n,), dtype=e.dtype).at[dst].add(w)
        denom = jnp.where(denom > 0, denom, 1.0)
        alpha = w / denom[dst]
        h_out = jnp.zeros((n, z.shape[1]), dtype=z.dtype).at[dst].add(alpha[:, None] * z[src])
        return h_out

    def _L1_gnn_ref(x, edge_index, edge_attr, msg_w, msg_b, self_w, self_b):
        import jax, jax.numpy as jnp
        import numpy as np
        N_NODES = 6250
        N_EDGES = 100000
        IN_DIM = 64
        EDGE_DIM = 32
        OUT_DIM = 64
        src = edge_index[0]
        dst = edge_index[1]
        n = x.shape[0]
        msg_in = jnp.concatenate([x[src], edge_attr], axis=1)
        messages = msg_in @ msg_w + msg_b
        agg = jax.ops.segment_sum(messages, dst, num_segments=n)
        deg = jax.ops.segment_sum(jnp.ones((dst.shape[0],), dtype=x.dtype), dst, num_segments=n)
        deg = jnp.maximum(deg, 1.0)[:, None]
        agg = agg / deg
        return x @ self_w + self_b + agg
    edge_index = jnp.stack([src, dst])
    x = _layernorm(x + _L0_gnn_ref(x, L0_gnn_fc_w, L0_gnn_attn_w, src, dst), axis=-1)
    x = _layernorm(x + _L1_gnn_ref(x, edge_index, edge_attr_32, L1_gnn_msg_w, L1_gnn_msg_b, L1_gnn_self_w, L1_gnn_self_b), axis=-1)
    return x

_drawn_inputs = setup_inputs


def setup_inputs(seed=0):
    import zlib

    import numpy as np

    out = dict(_drawn_inputs(seed))
    spreads = {}
    factors = {}
    for name, (base, spread) in spreads.items():
        noise = np.random.default_rng([zlib.crc32(name.encode()), seed]).standard_normal(out[name].shape)
        drawn = base * np.exp(spread * noise) if base else spread * noise
        out[name] = jnp.asarray(drawn.astype(out[name].dtype))
    for name, factor in factors.items():
        out[name] = (out[name] * factor).astype(out[name].dtype)
    return out
```

```python
import concourse.bass as bass
from concourse import mybir
from contextlib import ExitStack

ALU = mybir.AluOpType
ACT = mybir.ActivationFunctionType
AX_X = mybir.AxisListType.X
F32, BF16, I32 = mybir.dt.float32, mybir.dt.bfloat16, mybir.dt.int32

P = 128
BT = 112
GT = 28
QT = 4
WIN = QT * P
RG = 5
NEG = -1e38
SLOPE = 0.01
EPS = 1e-5


class Steps:

    def __init__(self, eng, sem, base=0):
        self.eng, self.sem, self.base, self.n = eng, sem, base, 0

    def did(self, ins):
        ins.then_inc(self.sem, 1)
        self.n += 1
        return self.n

    def wait(self, n=None):
        self.eng.wait_ge(self.sem, self.base + (self.n if n is None else n))


def gnn_layers(nc, x, src, dst, edge_attr, fc_w, attn_w, msg_w, msg_b, self_w, self_b, out):
    N, D = x.shape
    E = src.shape[0]
    DE = edge_attr.shape[1]
    NR = E // P
    NB = -(-NR // BT)
    NT = NB * BT
    LASTQ = NR - (NB - 1) * BT
    NG = BT // GT
    GB = GT // QT
    BB = BT // QT
    NHI = (N + P - 1) // P
    TAIL = N - (NHI - 1) * P
    RC = NHI
    CG = 7
    NCG = RC // CG
    ACCW = (RC + QT) * P
    NP = 125
    NJ = N // NP
    NCH = 4
    JC = NJ // NCH
    C0 = D + 2
    C1 = D + DE + 1
    R1N = NR // (RG * QT)
    NS = 3
    NCONST = 13
    assert NR * P == E and RC % CG == 0 and NP * NJ == N and D == 64
    assert R1N * RG * QT + QT + 1 == NR and BB % 2 == 0 and NB % 2 == 0 and NJ <= R1N
    assert (NCG * CG * P) <= ACCW and N + (NT - NR) + WIN <= ACCW

    h_dram = nc.dram_tensor("h_by_node", (N + P, D), F32).ap()
    a_dram = nc.dram_tensor("agg_by_node", (N + P, D), F32).ap()
    x1_dram = nc.dram_tensor("x1_by_node", (N, D), F32).ap()
    r0_dram = nc.dram_tensor("first_rank", (NB, BB), I32).ap()
    d_dram = nc.dram_tensor("tile_offset", (NB, BT), I32).ap()

    def alone(eng, s, value):
        eng.wait_ge(s, value)
        eng.sem_inc(passed, 1)

    with ExitStack() as ctx:
        def sb(name, shape, dt=F32):
            return ctx.enter_context(nc.sbuf_tensor(name, shape, dt))

        def psum(name, shape):
            return ctx.enter_context(nc.psum_tensor(name, shape, F32))

        def sem(name):
            return ctx.enter_context(nc.semaphore(name))

        acc = sb("acc", [P, ACCW])
        G = sb("G", [P, 2 * BT * D])
        idx = sb("idx", [P, NT], I32)
        idxg = sb("idxg", [P, 2 * NG, GT], I32)
        idg = sb("idg", [P, CG], I32)
        rel = sb("rel", [P, NT])
        dst_i = sb("dst_i", [BT, NB, P], I32)
        st = sb("st", [BT, NB, P], BF16)
        r0row = sb("r0row", [1, NB * BB], I32)
        drow = sb("drow", [1, NT], I32)
        prev_i = sb("prev_i", [BT, NB], I32)
        resets = sb("resets", [BT, NB, 3])
        pack3 = sb("pack3", [BT, 3])
        row3 = sb("row3", [1, 3, P])
        rowR = sb("rowR", [1, BT])
        inner = sb("inner", [BT, NB])
        cnt = sb("cnt", [BT, NB])
        st0 = sb("st0", [BT, NB])
        ident = sb("ident", [P, P])
        identb = sb("identb", [P, P], BF16)
        iota = sb("iota", [P, P])
        pidx = sb("pidx", [P, 1])
        dump = sb("dump", [P, 1])
        onesr = sb("onesr", [P, P])
        low = sb("low", [NB, NB])
        base0 = sb("base0", [NB, 1])
        r0i = sb("r0i", [NB, BT], I32)
        di = sb("di", [NB, BT], I32)
        srcf = sb("srcf", [BT, P])
        relrow = sb("relrow", [BT, P])
        fcw = sb("fcw", [D, D])
        acol = sb("acol", [D, 2])
        vsb = sb("vsb", [P, D])
        vdb = sb("vdb", [P, D])
        ED = sb("ED", [NHI, P])
        EDr = sb("EDr", [NHI, P])
        EDp = sb("EDp", [NHI, 3, P], BF16)
        R0 = sb("R0", [C0, C0])
        R1 = sb("R1", [C1, D + 1])
        SW = sb("SW", [D + 1, D])
        loi = sb("loi", [BT, P], I32)
        lof = sb("lof", [BT, P])
        hii = sb("hii", [BT, P], I32)
        hib = sb("hib", [BT, P], BF16)
        stdr = sb("stdr", [BT, P])
        negst = sb("negst", [BT, P + 1])
        loT = sb("loT", [P, BT])
        WD = sb("WD", [P, BT, 2])
        HY = sb("HY", [NHI, 2, WIN], BF16)
        L0 = sb("L0", [P, 2 * QT * C0 + QT * (P + D) + 5 * P + 2 * BT])
        OH = sb("OH", [NHI, 2, WIN], BF16)
        nhi = sb("nhi", [P, 1])
        zrow = sb("zrow", [1, WIN], BF16)
        es = sb("es", [P, BT])
        ed = sb("ed", [P, BT])
        fr = sb("fr", [1, 1])
        Kin = sb("Kin", [BT, 1])
        rowH = sb("rowH", [1, BT + 1])
        rowK = sb("rowK", [1, BT])
        Cin = sb("Cin", [BT, 1])
        rowC = sb("rowC", [1, BT + 1])
        Fs = sb("Fs", [C0, 1])
        fscale = sb("fscale", [C0, 1])
        U = sb("U", [P, NS, QT, P])
        nz = sb("nz", [P, CG])
        den = sb("den", [P, CG])
        rcp = sb("rcp", [P, CG])
        idT = sb("idT", [P, RC], I32)
        mean = sb("mean", [NP, JC])
        var = sb("var", [NP, JC])
        sd = sb("sd", [NP, JC])
        rstd = sb("rstd", [NP, JC])
        eps = sb("eps", [P, 1])
        xs = sb("xs", [NP, D])
        xT = sb("xT", [D + 1, NP])

        HB = psum("HB", [P, 1024])
        EDP = psum("EDP", [P, 1024])
        MP = psum("MP", [P, 1536])
        PF = psum("PF", [P, 512])

        cT, sT, cum, tmp0 = [acc[0:NB, 11776 + k * BT:11776 + (k + 1) * BT] for k in range(4)]
        cut = [0]

        def part(parts, *shape):
            size = 1
            for k in shape:
                size *= k
            v = L0[0:parts, cut[0]:cut[0] + size]
            cut[0] += size
            if len(shape) == 2:
                v = v.rearrange("p (a b) -> p a b", a=shape[0])
            if len(shape) == 3:
                v = v.rearrange("p (a b c) -> p a b c", a=shape[0], b=shape[1])
            return v

        SR = part(P, 2, QT, C0)
        selj = part(P, QT, P)
        esx = part(P, QT, D)
        F1, F2, M, wr, Bh = [part(BT, P) for _ in range(5)]
        S0, S = part(P, BT), part(P, BT)
        ring = L0[:, 0:RG * QT * C1].rearrange("p (t c) -> p t c", c=C1)
        accS = U[:, :, :, :].rearrange("p s j r -> p (s j r)")[0:C1, 0:CG * P]
        Gt = G[:, :].rearrange("p (t d) -> p t d", d=D)
        src_i = acc[0:BT, 8192:8192 + NB * P].bitcast(I32).rearrange("q (b e) -> q b e", e=P)
        xhi = acc[0:NHI, 0:P * D]
        hst = G[:, 0:RC * D].rearrange("p (c d) -> p c d", d=D)
        ND = NJ * D
        x1v = G[0:NP, ND:2 * ND].rearrange("p (j d) -> p j d", d=D)
        yv = G[0:NP, 0:ND].rearrange("p (j d) -> p j d", d=D)
        hst2 = G[:, ND:ND + RC * D].rearrange("p (c d) -> p c d", d=D)
        hv = acc[0:NP, 0:ND].rearrange("p (j d) -> p j d", d=D)
        sqv = acc[0:NP, ND:ND + JC * D].rearrange("p (j d) -> p j d", d=D)
        MPb = [MP[:, 512 * k:512 * (k + 1)] for k in range(3)]
        B = [HB[:, 0:512], HB[:, 512:1024], EDP[:, 0:512], EDP[:, 512:1024], PF[:, :]]
        HBb = [B[0], B[1]]
        EDb = [B[k].rearrange("p (j r) -> p j r", r=P) for k in (2, 3)]
        LO_T, ID_T, ROWS = B[0][:, 0:BT], B[1][:, 0:BT], B[2][0:1, 0:3 * P].rearrange("o (k q) -> o k q", k=3)
        S_T, TAILR, HEADR, W_T = B[2][0:BT, 0:P], B[0][0:1, 0:BT], B[1][0:1, 0:BT], B[3][:, 0:BT]
        CINC, CINK, FB = B[0][0:BT, 0:1], B[1][0:BT, 0:1], B[4][0:C0, 0:1]
        HP = [HB[:, 0:CG * C0].rearrange("p (j c) -> p j c", c=C0),
              HB[:, 512:512 + CG * C0].rearrange("p (j c) -> p j c", c=C0)]
        HQ = [HB[:, 0:CG * (D + 1)].rearrange("p (j c) -> p j c", c=D + 1),
              HB[:, 512:512 + CG * (D + 1)].rearrange("p (j c) -> p j c", c=D + 1)]

        passed, rescaled = sem("passed"), sem("rescaled")
        idx_copied, id_copied, idx1_ready = sem("idx_copied"), sem("id_copied"), sem("idx1_ready")
        ld_edges, ld_prev, ld_w, ld_xhi = sem("ld_edges"), sem("ld_prev"), sem("ld_w"), sem("ld_xhi")
        prev_set, xhi_set, consts, consts2 = sem("prev_set"), sem("xhi_set"), sem("consts"), sem("consts2")
        pro, pro_t, idx_ready = sem("pro"), sem("pro_t"), sem("idx_ready")
        set_d, set_p, acc_zero, acc_zero1 = sem("set_d"), sem("set_p"), sem("acc_zero"), sem("acc_zero1")
        r0_done, r0_st, r0_ld, tab0 = sem("r0_done"), sem("r0_st"), sem("r0_ld"), sem("tab0")
        gathered = [sem(f"gathered{g}") for g in range(NG)]
        prep, prep_t = sem("prep"), sem("prep_t")
        pads, hb_used = sem("pads"), sem("hb_used")
        hb_ready, onehot_hi, ed_ready, ed_free, es_prod, es_ready = (
            sem("hb_ready"), sem("onehot_hi"), sem("ed_ready"), sem("ed_free"), sem("es_prod"), sem("es_ready"))
        sm, sm_t, exp_ready = sem("sm"), sem("sm_t"), sem("exp_ready")
        rows_scaled, onehots, agg, mp_free = sem("rows_scaled"), sem("onehots"), sem("agg"), sem("mp_free")
        stg, hp_ready, hp_used, hst_ready, scat = sem("stg"), sem("hp_ready"), sem("hp_used"), sem("hst_ready"), sem("scat")
        fin_d = sem("fin_d")
        ld_x, ld_h, ln, ln_sd, x1_ready, x1_st = sem("ld_x"), [sem(f"ld_h{c}") for c in range(NCH)], sem("ln"), sem("ln_sd"), sem("x1_ready"), sem("x1_st")
        ring_ones, sw_ready = sem("ring_ones"), sem("sw_ready")
        g1 = [sem(f"g1_{s}") for s in range(RG)]
        at1 = [sem(f"at1_{s}") for s in range(RG)]
        u1, agg1, mp1_free = sem("u1"), sem("agg1"), sem("mp1_free")
        xs_r, xst_r, xT_r, y_p, y_r = sem("xs_r"), sem("xst_r"), sem("xT_r"), sem("y_p"), sem("y_r")
        stg1, hq_ready, hq_used, hst2_ready, scat2, fin2 = (
            sem("stg1"), sem("hq_ready"), sem("hq_used"), sem("hst2_ready"), sem("scat2"), sem("fin2"))
        ld_a = [sem(f"ld_a{c}") for c in range(NCH)]
        ln2, ln2_sd, y_out, out_st = sem("ln2"), sem("ln2_sd"), sem("y_out"), sem("out_st")

        block = ctx.enter_context(nc.Block())

        def by_tile(e):
            n = (NB - 1) * BT * P
            return e[0:n].rearrange("(b q e) -> q b e", q=BT, e=P), e[n:E].rearrange("(q e) -> q e", e=P)

        at_t = edge_attr.rearrange("(t e) f -> e t f", e=P)

        def node_order(t):
            return t[0:N, :].rearrange("(p j) d -> p j d", p=NP)

        @block.sync
        def _(sp):
            with nc.allow_non_contiguous_dma(reason="one word per tile, and columns of weights"):
                sp.wait_ge(pads, 2)
                for t, e in ((src_i, src), (dst_i[:, :, :], dst)):
                    full, rest = by_tile(e)
                    sp.dma_start(t[:, 0:NB - 1, :], full).then_inc(ld_edges, 16)
                    sp.dma_start(t[0:LASTQ, NB - 1, :], rest).then_inc(ld_edges, 16)
                full, rest = by_tile(dst)
                sp.wait_ge(prev_set, 1)
                sp.dma_start(prev_i[1:BT, 0:NB - 1].unsqueeze(2), full[0:BT - 1, :, P - 1:P]).then_inc(ld_prev, 16)
                sp.dma_start(prev_i[0:1, 1:NB].unsqueeze(2), full[BT - 1:BT, :, P - 1:P]).then_inc(ld_prev, 16)
                sp.dma_start(prev_i[1:LASTQ, NB - 1:NB], rest[0:LASTQ - 1, P - 1:P]).then_inc(ld_prev, 16)
                sp.dma_start(fcw[:, :], fc_w).then_inc(ld_w, 16)
                sp.dma_start(acol[:, 0:1], attn_w[0, 0:D].unsqueeze(1)).then_inc(ld_w, 16)
                sp.dma_start(acol[:, 1:2], attn_w[0, D:2 * D].unsqueeze(1)).then_inc(ld_w, 16)
            sp.wait_ge(xhi_set, 1)
            sp.dma_start(xhi[0:NHI - 1, :], x[0:(NHI - 1) * P, :].rearrange("(h l) d -> h (l d)", l=P)).then_inc(ld_xhi, 16)
            sp.dma_start(xhi[NHI - 1:NHI, 0:TAIL * D],
                         x[(NHI - 1) * P:N, :].rearrange("(h l) d -> h (l d)", h=1)).then_inc(ld_xhi, 16)
            sp.dma_start(R1[0:D + DE, 0:D], msg_w).then_inc(ld_w, 16)
            sp.dma_start(R1[D + DE:C1, 0:D], msg_b.unsqueeze(0)).then_inc(ld_w, 16)
            sp.dma_start(SW[0:D, :], self_w).then_inc(ld_w, 16)
            sp.dma_start(SW[D:D + 1, :], self_b.unsqueeze(0)).then_inc(ld_w, 16)
            sp.wait_ge(acc_zero, 1)
            for t in (h_dram, a_dram):
                sp.dma_start(node_order(t), hv).then_inc(tab0, 16)
            sp.wait_ge(r0_done, 1)
            with nc.allow_non_contiguous_dma(reason="first tile of each batch"):
                sp.dma_start(r0_dram.unsqueeze(2), r0i[:, :].rearrange("b (n j) -> b n j", j=QT)[:, :, 0:1]).then_inc(r0_st, 16)
            sp.dma_start(d_dram, di[:, :]).then_inc(r0_st, 16)
            sp.wait_ge(r0_st, 32)
            sp.dma_start(r0row[0:1, :], r0_dram.rearrange("b t -> (b t)").unsqueeze(0)).then_inc(r0_ld, 16)
            sp.dma_start(drow[0:1, :], d_dram.rearrange("b t -> (b t)").unsqueeze(0)).then_inc(r0_ld, 16)
            sp.wait_ge(rows_scaled, NB * BB + 2 * BB)
            sp.dma_start(x1v, node_order(x)).then_inc(ld_x, 16)
            sp.wait_ge(scat, RC * 16)
            sp.wait_ge(stg, 2 * NCG)
            for c in range(NCH):
                sp.dma_start(hv[:, c * JC:(c + 1) * JC, :],
                             node_order(h_dram)[:, c * JC:(c + 1) * JC, :]).then_inc(ld_h[c], 16)
            for c in range(NCH):
                sp.wait_ge(x1_ready, c + 1)
                sp.dma_start(node_order(x1_dram)[:, c * JC:(c + 1) * JC, :],
                             x1v[:, c * JC:(c + 1) * JC, :]).then_inc(x1_st, 16)
            def load_attr(n, s, tiles):
                sp.wait_ge(agg1, n + 1)
                sp.dma_start(ring[:, s * QT:s * QT + tiles, D:D + DE],
                             at_t[:, bass.ds(n * QT, tiles), :]).then_inc(at1[s], 16)

            with sp.Fori(0, R1N) as i:
                for s in range(RG):
                    load_attr(i * RG + s, s, QT)
            load_attr(R1N * RG, 0, QT)
            load_attr(R1N * RG + 1, 1, 1)
            sp.wait_ge(scat2, RC * 16)
            sp.wait_ge(stg1, 2 * NCG)
            for c in range(NCH):
                sp.dma_start(hv[:, c * JC:(c + 1) * JC, :],
                             node_order(a_dram)[:, c * JC:(c + 1) * JC, :]).then_inc(ld_a[c], 16)
            for c in range(NCH):
                sp.wait_ge(y_out, c + 1)
                sp.dma_start(node_order(out)[:, c * JC:(c + 1) * JC, :],
                             yv[:, c * JC:(c + 1) * JC, :]).then_inc(out_st, 16)
            sp.wait_ge(out_st, NCH * 16)

        @block.gpsimd
        def _(g):
            c = Steps(g, consts)
            g.memset(src_i, 0).then_inc(pads, 1)
            g.wait_ge(pads, 1)
            g.memset(dst_i[:, :, :], -1).then_inc(pads, 1)
            g.wait_ge(pads, 2)
            g.memset(prev_i[:, :], -2).then_inc(prev_set, 1)
            g.wait_ge(prev_set, 1)
            g.memset(xhi[96:NHI, :], 0.0).then_inc(xhi_set, 1)
            g.wait_ge(xhi_set, 1)
            for tile, value in ((onesr, 1.0), (eps, EPS), (rowC, NEG), (rowH, NEG), (relrow, 0.0), (negst, 0.0), (fscale, 1.0),
                                (ident, 0.0)):
                c.did(g.memset(tile[:, :], value))
                c.wait()
            for tile, pattern, first, by_partition in ((iota, [[1, P]], 0, 0), (pidx, [[0, 1]], 0, 1), (dump, [[0, 1]], N, 1)):
                c.did(g.iota(tile[:, :], pattern=pattern, base=first, channel_multiplier=by_partition,
                             allow_small_or_imprecise_dtypes=True))
                c.wait()
            c.did(g.affine_select(out=ident[:, :], in_=ident[:, :], compare_op=ALU.not_equal, fill=1.0,
                                  base=0, pattern=[[-1, P]], channel_multiplier=1))
            c.wait()
            c.did(g.affine_select(out=fscale[:, :], in_=fscale[:, :], compare_op=ALU.not_equal, fill=0.0,
                                  base=-(D + 1), pattern=[[0, 1]], channel_multiplier=1))
            assert c.n == NCONST

            def gather_block(b, half):
                alone(g, pro, (b + 1) * 5)
                for k in range(NG):
                    alone(g, rows_scaled, b * BB + (k + 1) * GB)
                    alone(g, es_ready, b * BB + (k + 1) * GB + 1)
                    g.tensor_copy(idxg[:, half * NG + k, :], idx[:, bass.ds(b * BT + k * GT, GT)]).then_inc(idx_copied, 1)
                    alone(g, idx_copied, b * NG + k + 1)
                    for j in range(GT):
                        g.indirect_dma_start(Gt[:, half * BT + k * GT + j, :], None, x[:, :],
                                             bass.IndirectOffsetOnAxis(ap=idxg[:, half * NG + k, j:j + 1], axis=0)
                                             ).then_inc(gathered[k], 16)

            with g.Fori(0, NB // 2) as b2:
                for half in range(2):
                    gather_block(b2 * 2 + half, half)

            g.wait_ge(tab0, 32)
            for c7 in range(NCG):
                g.wait_ge(hst_ready, c7 + 1)
                for j in range(c7 * CG, (c7 + 1) * CG):
                    g.indirect_dma_start(h_dram[:, :], bass.IndirectOffsetOnAxis(ap=idT[:, j:j + 1], axis=0),
                                         hst[:, j, :], None).then_inc(scat, 16)

            g.wait_ge(x1_st, NCH * 16)
            g.wait_ge(ring_ones, 1)
            def gather1(n, s, tiles):
                    alone(g, idx1_ready, n + 1)
                    for j in range(tiles):
                        g.indirect_dma_start(ring[:, s * QT + j, 0:D], None, x1_dram[:, :],
                                             bass.IndirectOffsetOnAxis(ap=idxg[:, s, j:j + 1], axis=0)
                                             ).then_inc(g1[s], 16)

            with g.Fori(0, R1N) as i:
                for s in range(RG):
                    gather1(i * RG + s, s, QT)
            gather1(R1N * RG, 0, QT)
            gather1(R1N * RG + 1, 1, 1)

            for c7 in range(NCG):
                g.wait_ge(hst2_ready, c7 + 1)
                for j in range(c7 * CG, (c7 + 1) * CG):
                    g.indirect_dma_start(a_dram[:, :], bass.IndirectOffsetOnAxis(ap=idT[:, j:j + 1], axis=0),
                                         hst2[:, j, :], None).then_inc(scat2, 16)

        @block.vector
        def _(v):
            for free, buffers in ((es_ready, 1 + BB), (ed_free, 2), (rows_scaled, 2 * BB), (agg, 2), (agg1, RG),
                                  (mp_free, 2), (mp1_free, 2), (hb_used, 2), (onehot_hi, 2), (ed_ready, 2)):
                v.sem_inc(free, buffers)

            d = Steps(v, set_d)
            v.wait_ge(consts, NCONST)
            d.did(v.tensor_copy(identb[:, :], ident[:, :]))
            d.did(v.tensor_tensor(low[:, :], iota[0:NB, 0:NB], pidx[0:NB, 0:1].to_broadcast([NB, NB]), ALU.is_gt))
            v.memset(row3[:, :, :], 0.0)
            v.memset(zrow[:, :], 0.0)
            v.tensor_scalar(nhi[:, :], pidx[:, :], -1.0, None, ALU.mult)
            v.wait_ge(ld_edges, 64)
            v.wait_ge(ld_prev, 48)
            v.tensor_tensor(st[:, :, 1:P], dst_i[:, :, 1:P], dst_i[:, :, 0:P - 1], ALU.not_equal)
            v.tensor_tensor(st[:, :, 0:1], dst_i[:, :, 0:1], prev_i[:, :].unsqueeze(2), ALU.not_equal)
            d.did(v.tensor_tensor(st0[:, :].unsqueeze(2), dst_i[:, :, 0:1], prev_i[:, :].unsqueeze(2), ALU.not_equal))
            d.wait()
            with v.Fori(0, NB) as b:
                p = Steps(v, pro, b * 5)
                q = Steps(v, pro_t, b * 2)
                p.did(v.tensor_copy(srcf[:, :], src_i[:, b, :]))
                p.did(v.tensor_tensor_scan(relrow[:, 1:P], onesr[0:BT, 0:P - 1], st[:, b, 1:P], 0.0, ALU.mult, ALU.add))
                p.wait()
                p.did(v.tensor_tensor(cnt[:, bass.ds(b, 1)], relrow[:, P - 1:P], st0[:, bass.ds(b, 1)], ALU.add))
                q.wait(1)
                p.did(v.tensor_copy(idx[:, bass.ds(b * BT, BT)], B[0][:, 0:BT]))
                q.wait(2)
                p.did(v.tensor_copy(rel[:, bass.ds(b * BT, BT)], B[1][:, 0:BT]))
                p.wait()

            v.wait_ge(pro, NB * 5)
            v.memset(rel[:, NR:NT], -1.0)
            v.tensor_tensor(inner[:, :], cnt[:, :], st0[:, :], ALU.subtract)
            v.tensor_scalar(resets[:, :, 0], cnt[:, :], 0.0, NEG, ALU.is_gt, ALU.mult)
            d.did(v.tensor_scalar(resets[:, :, 2], st0[:, :], NEG, None, ALU.mult))
            d.wait()
            v.tensor_scalar(resets[:, :, 1], inner[:, :], 0.0, NEG, ALU.is_gt, ALU.mult)
            v.wait_ge(set_p, 2)
            v.tensor_copy(cT[:, :], B[0][0:NB, 0:BT])
            d.did(v.tensor_copy(sT[:, :], B[0][0:NB, 128:128 + BT]))
            d.wait()
            d.did(v.tensor_tensor_scan(cum[:, :], onesr[0:NB, 0:BT], cT[:, :], 0.0, ALU.mult, ALU.add))
            d.wait()
            d.did(v.tensor_tensor(tmp0[:, :], cum[:, :], cT[:, :], ALU.subtract))
            v.wait_ge(set_p, 3)
            d.did(v.tensor_copy(base0[:, :], B[1][0:NB, 0:1]))
            d.wait()
            d.did(v.tensor_tensor(cum[:, :], tmp0[:, :], sT[:, :], ALU.add))
            d.wait()
            v.tensor_scalar(r0i[:, :], cum[:, :], base0[:, 0:1], -1.0, ALU.add, ALU.add)
            cum3 = cum[:, :].rearrange("b (n j) -> b n j", j=QT)
            v.tensor_tensor(di[:, :].rearrange("b (n j) -> b n j", j=QT), cum3,
                            cum3[:, :, 0:1].to_broadcast([NB, BB, QT]), ALU.subtract).then_inc(r0_done, 1)

            v.wait_ge(set_p, 6)
            v.tensor_copy(vsb[:, :], B[2][:, 0:D])
            v.tensor_copy(R0[:, :], ident[0:C0, 0:C0])
            v.tensor_copy(R1[:, D:D + 1], ident[0:C1, C1 - 1:C1])
            d.did(v.tensor_copy(vdb[:, :], B[2][:, 128:128 + D]))
            d.wait()
            v.wait_ge(set_p, 6)
            v.tensor_copy(R0[0:D, 0:D], B[2][0:D, 256:256 + D])
            v.wait_ge(ld_xhi, 32)
            xh3 = xhi.rearrange("h (l d) -> h l d", d=D)
            d.did(v.tensor_tensor(xh3, xh3, vdb[0:NHI, :].unsqueeze(1).to_broadcast([NHI, P, D]), ALU.mult))
            d.wait()
            d.did(v.tensor_reduce(ED[:, :], xh3, AX_X, ALU.add))
            d.wait()
            d.did(v.tensor_copy(EDp[:, 0, :], ED[:, :]))
            d.wait()
            d.did(v.tensor_tensor(EDr[:, :], ED[:, :], EDp[:, 0, :], ALU.subtract))
            d.wait()
            d.did(v.tensor_copy(EDp[:, 1, :], EDr[:, :]))
            d.wait()
            d.did(v.tensor_tensor(ED[:, :], EDr[:, :], EDp[:, 1, :], ALU.subtract))
            d.wait()
            d.did(v.tensor_copy(EDp[:, 2, :], ED[:, :]))
            v.memset(acc[:, :], 0.0).then_inc(acc_zero, 1)

            with v.Fori(0, NB) as b:
                p = Steps(v, prep, b * 11)
                p.did(v.tensor_scalar(loi[:, :], dst_i[:, b, :], P - 1, None, ALU.bitwise_and))
                p.did(v.tensor_scalar(hii[:, :], dst_i[:, b, :], 7, None, ALU.logical_shift_right))
                p.wait()
                p.did(v.tensor_copy(lof[:, :], loi[:, :]))
                p.did(v.tensor_copy(hib[:, :], hii[:, :]))
                p.did(v.tensor_tensor(stdr[:, :], dst_i[:, b, :], st[:, b, :], ALU.mult))
                p.did(v.tensor_scalar(negst[:, 0:P], st[:, b, :], NEG, None, ALU.mult))
                p.did(v.tensor_copy(pack3[:, :], resets[:, b, :]))
                v.wait_ge(prep_t, b * 3 + 1)
                p.did(v.tensor_copy(loT[:, :], LO_T))
                v.wait_ge(prep_t, b * 3 + 2)
                p.did(v.tensor_copy(WD[:, :, 1], ID_T))
                v.wait_ge(prep_t, b * 3 + 3)
                p.did(v.tensor_copy(row3[:, :, 0:BT], ROWS[:, :, 0:BT]))
                p.wait()
                p.did(v.tensor_tensor(rowR[:, :], row3[:, 1, 0:BT], row3[:, 2, 1:BT + 1], ALU.add))
                p.wait()
                for i in range(BB):
                    n = b * BB + i
                    q0 = i * QT

                    def pick(j):
                        return v.scalar_tensor_tensor(out=selj[:, j, :], in0=iota[:, :], scalar=loT[:, q0 + j:q0 + j + 1],
                                                      in1=EDb[i % 2][:, j, :], op0=ALU.is_equal, op1=ALU.mult,
                                                      accum_out=ed[:, q0 + j:q0 + j + 1])

                    if i % GB == 0:
                        v.wait_ge(gathered[i // GB], (b + 1) * GT * 16)
                    v.wait_ge(es_ready, n + 1 + BB)
                    v.tensor_tensor(esx[:, :, :], Gt[:, bass.ds((b % 2) * BT + q0, QT), :],
                                    vsb[:, :].unsqueeze(1).to_broadcast([P, QT, D]), ALU.mult).then_inc(es_prod, 1)
                    v.wait_ge(ed_free, n + 2)
                    v.wait_ge(ed_ready, n + 3)
                    pick(0)
                    pick(1)
                    v.wait_ge(es_prod, n + 1)
                    v.tensor_reduce(es[:, q0:q0 + QT], esx[:, :, :], AX_X, ALU.add).then_inc(es_ready, 1)
                    pick(2)
                    pick(3).then_inc(ed_free, 1)
                p = Steps(v, sm, b * 14)
                v.wait_ge(ed_free, (b + 1) * BB + 2)
                p.did(v.tensor_tensor(S0[:, :], es[:, :], ed[:, :], ALU.add))
                p.wait()
                p.did(v.scalar_tensor_tensor(out=S[:, :], in0=S0[:, :], scalar=SLOPE, in1=S0[:, :],
                                             op0=ALU.mult, op1=ALU.max))
                v.wait_ge(sm_t, b * 7 + 1)
                p.did(v.tensor_tensor_scan(F1[:, :], negst[:, 0:P], S_T, NEG, ALU.add, ALU.max))
                p.did(v.tensor_tensor_scan(Bh[:, P - 1::-1], negst[:, P:0:-1], S_T[:, P - 1::-1], NEG, ALU.add, ALU.max))
                v.wait_ge(sm_t, b * 7 + 2)
                p.did(v.tensor_tensor_scan(rowC[0:1, 1:BT + 1], row3[:, 0, 0:BT], TAILR, rowC[0:1, 0:1], ALU.add, ALU.max))
                v.wait_ge(sm_t, b * 7 + 3)
                p.did(v.tensor_tensor_scan(rowH[0:1, BT - 1::-1], rowR[:, BT - 1::-1], HEADR[:, BT - 1::-1], NEG, ALU.add, ALU.max))
                p.wait()
                p.did(v.tensor_tensor(rowK[:, :], rowH[0:1, 1:BT + 1], row3[:, 2, 1:BT + 1], ALU.add))
                v.wait_ge(sm_t, b * 7 + 4)
                p.did(v.tensor_copy(Cin[:, :], CINC))
                v.wait_ge(sm_t, b * 7 + 5)
                p.did(v.tensor_copy(Kin[:, :], CINK))
                p.did(v.tensor_copy(rowC[0:1, 0:1], rowC[0:1, BT:BT + 1]))
                p.wait(9)
                p.did(v.tensor_tensor_scan(F2[:, :], negst[:, 0:P], S_T, Cin[:, 0:1], ALU.add, ALU.max))
                p.wait()
                p.did(v.tensor_tensor_scan(M[:, P - 1::-1], negst[:, P:0:-1], F2[:, P - 1::-1], Kin[:, 0:1], ALU.add, ALU.max))
                p.wait()
                p.did(v.tensor_tensor(wr[:, :], S_T, M[:, :], ALU.subtract))
                p.did(v.tensor_scalar(fr[:, :], Cin[0:1, :], M[0:1, 0:1], 0.0, ALU.subtract, ALU.min))
                alone(v, exp_ready, b * 2 + 1)
                with v.Fori(0, BB // 2) as i:
                    for sl in range(2):
                        n = b * BB + i * 2 + sl
                        q0 = i * 2 * QT + sl * QT
                        v.wait_ge(agg, n + 1)
                        v.tensor_tensor(SR[:, sl, :, 0:D], Gt[:, bass.ds((b % 2) * BT + q0, QT), :],
                                        WD[:, bass.ds(q0, QT), 0:1].to_broadcast([P, QT, D]), ALU.mult).then_inc(rows_scaled, 1)
                        v.tensor_copy(SR[:, sl, :, D:C0], WD[:, bass.ds(q0, QT), :])
                        v.tensor_tensor(U[:, sl, :, :], iota[:, :].unsqueeze(1).to_broadcast([P, QT, P]),
                                        rel[:, bass.ds(b * BT + q0, QT)].unsqueeze(2).to_broadcast([P, QT, P]),
                                        ALU.is_equal).then_inc(onehots, 1)

            with v.Fori(0, NCG // 2) as i:
                for k in range(2):
                    c7 = i * 2 + k
                    f = Steps(v, fin_d, c7 * 4)
                    v.wait_ge(hp_ready, c7 + 1)
                    f.did(v.tensor_scalar(nz[:, :], HP[k][:, :, D], 0.0, None, ALU.is_equal))
                    f.wait()
                    f.did(v.tensor_tensor(den[:, :], HP[k][:, :, D], nz[:, :], ALU.add))
                    f.wait()
                    f.did(v.reciprocal(rcp[:, :], den[:, :]))
                    f.did(v.scalar_tensor_tensor(out=idT[:, bass.ds(c7 * CG, CG)], in0=nz[:, :], scalar=dump[:, 0:1],
                                                 in1=HP[k][:, :, D + 1], op0=ALU.mult, op1=ALU.add))
                    f.wait()
                    v.tensor_tensor(hst[:, bass.ds(c7 * CG, CG), :], HP[k][:, :, 0:D],
                                    rcp[:, :].unsqueeze(2).to_broadcast([P, CG, D]), ALU.mult).then_inc(hst_ready, 1)

            def layer_norm(a, r, c, s, s_sd, done):
                ac, rc = a[:, c * JC:(c + 1) * JC, :], r[:, c * JC:(c + 1) * JC, :]
                f = Steps(v, s, c * 7)
                f.did(v.tensor_tensor(ac, ac, rc, ALU.add))
                f.wait()
                f.did(v.tensor_reduce(mean[:, :], ac, AX_X, ALU.add))
                f.wait()
                f.did(v.scalar_tensor_tensor(out=ac, in0=mean[:, :].unsqueeze(2).to_broadcast([NP, JC, D]),
                                             scalar=-1.0 / D, in1=ac, op0=ALU.mult, op1=ALU.add))
                f.wait()
                f.did(v.tensor_tensor(sqv, ac, ac, ALU.mult))
                f.wait()
                f.did(v.tensor_reduce(var[:, :], sqv, AX_X, ALU.add))
                v.wait_ge(s_sd, c + 1)
                f.did(v.reciprocal(rstd[:, :], sd[:, :]))
                f.wait()
                f.did(v.tensor_tensor(ac, ac, rstd[:, :].unsqueeze(2).to_broadcast([NP, JC, D]), ALU.mult))
                f.wait()
                v.sem_inc(done, 1)

            v.wait_ge(ld_x, 16)
            for c in range(NCH):
                v.wait_ge(ld_h[c], 16)
                layer_norm(x1v, hv, c, ln, ln_sd, x1_ready)
            v.memset(ring[:, :, D + DE:C1], 1.0).then_inc(ring_ones, 1)
            v.memset(xT[D:D + 1, :], 1.0).then_inc(sw_ready, 1)
            v.memset(acc[:, :], 0.0).then_inc(acc_zero1, 1)

            def onehots1(n, s, tiles):
                v.wait_ge(agg1, n + 1)
                v.tensor_copy(idxg[:, s, 0:tiles], idx[:, bass.ds(n * QT, tiles)]).then_inc(idx1_ready, 1)
                v.wait_ge(agg1, n + RG - 1)
                v.tensor_tensor(U[:, s % NS, 0:tiles, :], iota[:, :].unsqueeze(1).to_broadcast([P, tiles, P]),
                                rel[:, bass.ds(n * QT, tiles)].unsqueeze(2).to_broadcast([P, tiles, P]),
                                ALU.is_equal).then_inc(u1, 1)

            def round1(i, self_term):
                for s in range(RG):
                    onehots1(i * RG + s, s, QT)
                    if self_term and s == 1:
                        v.wait_ge(xst_r, i + 1)
                        v.tensor_copy(xT[0:D, :], B[0][0:D, 0:NP]).then_inc(xT_r, 1)
                    if self_term and s == 3:
                        v.wait_ge(y_p, i + 1)
                        v.tensor_tensor(yv[:, i, :], B[1][0:NP, 0:D], x1v[:, i, :], ALU.add).then_inc(y_r, 1)

            with v.Fori(0, NJ) as i:
                round1(i, True)
            with v.Fori(NJ, R1N) as i:
                round1(i, False)
            onehots1(R1N * RG, 0, QT)
            onehots1(R1N * RG + 1, 1, 1)

            v.wait_ge(y_r, NJ)
            with v.Fori(0, NCG // 2) as i:
                for k in range(2):
                    c7 = i * 2 + k
                    f = Steps(v, fin2, c7 * 2)
                    v.wait_ge(hq_ready, c7 + 1)
                    f.did(v.tensor_scalar(den[:, :], HQ[k][:, :, D], 1.0, None, ALU.max))
                    f.wait()
                    f.did(v.reciprocal(rcp[:, :], den[:, :]))
                    f.wait()
                    v.tensor_tensor(hst2[:, bass.ds(c7 * CG, CG), :], HQ[k][:, :, 0:D],
                                    rcp[:, :].unsqueeze(2).to_broadcast([P, CG, D]), ALU.mult).then_inc(hst2_ready, 1)
            for c in range(NCH):
                v.wait_ge(ld_a[c], 16)
                layer_norm(yv, hv, c, ln2, ln2_sd, y_out)

        @block.tensor
        def _(t):
            def offsets(n):
                _, values = nc.values_load_multi_w_load_instructions(
                    drow[0:1, bass.ds(n * QT, QT)], engines=(mybir.EngineType.PE,), min_val=0, max_val=WIN - P)
                return values

            def add_batch(bank, cols, rows, sl, offs):
                t.matmul(bank[0:cols, :], zrow[0:1, 0:cols], zrow[0:1, :], start=True, stop=False, skip_group_check=True)
                for j, r in enumerate(rows):
                    mm = t.matmul(bank[0:cols, bass.ds(offs[j], P)], r, U[:, sl, j, :], start=False,
                                  stop=(j == len(rows) - 1), skip_group_check=True)
                return mm

            t.wait_ge(consts, NCONST)
            with t.Fori(0, NB) as b:
                t.wait_ge(pro, b * 5 + 1)
                t.transpose(B[0][:, 0:BT], srcf[:, :], ident[0:BT, 0:BT]).then_inc(pro_t, 1)
                t.wait_ge(pro, b * 5 + 2)
                t.transpose(B[1][:, 0:BT], relrow[:, :], ident[0:BT, 0:BT]).then_inc(pro_t, 1)
            t.wait_ge(pro, NB * 5)
            t.wait_ge(set_d, 3)
            t.transpose(B[0][0:NB, 0:BT], cnt[:, :], ident[0:BT, 0:BT]).then_inc(set_p, 1)
            t.transpose(B[0][0:NB, 128:128 + BT], st0[:, :], ident[0:BT, 0:BT]).then_inc(set_p, 1)
            t.wait_ge(set_d, 6)
            t.matmul(B[1][0:NB, 0:1], low[:, :], cum[:, BT - 1:BT], start=True, stop=True).then_inc(set_p, 1)
            t.wait_ge(ld_w, 7 * 16)
            t.matmul(B[2][:, 0:D], acol[:, 0:1].to_broadcast([D, P]), fcw[:, :], start=True, stop=True).then_inc(set_p, 1)
            t.matmul(B[2][:, 128:128 + D], acol[:, 1:2].to_broadcast([D, P]), fcw[:, :], start=True, stop=True).then_inc(set_p, 1)
            t.transpose(B[2][0:D, 256:256 + D], fcw[:, :], ident[0:D, 0:D]).then_inc(set_p, 1)

            t.wait_ge(acc_zero, 1)
            t.wait_ge(r0_ld, 32)
            with t.Fori(0, NB) as b:
                t.wait_ge(prep, b * 11 + 7)
                t.transpose(LO_T, lof[:, :], ident[0:BT, 0:BT]).then_inc(prep_t, 1)
                t.transpose(ID_T, stdr[:, :], ident[0:BT, 0:BT]).then_inc(prep_t, 1)
                for k in range(3):
                    mm = t.matmul(ROWS[:, k, 0:BT], pack3[:, k:k + 1], ident[0:BT, 0:BT], start=True, stop=True)
                mm.then_inc(prep_t, 1)
                alone(t, prep, b * 11 + 10)

                def spread_hi(n, q0, sl):
                    t.wait_ge(hb_used, n + 1)
                    for j in range(QT):
                        mm = t.matmul(HBb[sl][0:NHI, j * P:(j + 1) * P],
                                      identb[0:BT, bass.ds(q0 + j, 1)].to_broadcast([BT, NHI]),
                                      hib[:, :], start=True, stop=True)
                    mm.then_inc(hb_ready, 1)

                def choose_hi(n, sl):
                    t.wait_ge(onehot_hi, n + 3)
                    t.wait_ge(ed_free, n + 1)
                    for j in range(QT):
                        for c in range(3):
                            mm = t.matmul(EDb[sl][:, j, :], OH[:, sl, j * P:(j + 1) * P], EDp[:, c, :],
                                          start=(c == 0), stop=(c == 2))
                    mm.then_inc(ed_ready, 1)

                spread_hi(b * BB, 0, 0)
                with t.Fori(0, BB // 2 - 1) as i:
                    for sl in range(2):
                        n = b * BB + i * 2 + sl
                        spread_hi(n + 1, i * 2 * QT + (sl + 1) * QT, 1 - sl)
                        choose_hi(n, sl)
                spread_hi((b + 1) * BB - 1, BT - QT, 1)
                choose_hi((b + 1) * BB - 2, 0)
                choose_hi((b + 1) * BB - 1, 1)
                t.wait_ge(sm, b * 14 + 2)
                t.transpose(S_T, S[:, :], ident[:, :]).then_inc(sm_t, 1)
                t.wait_ge(sm, b * 14 + 3)
                t.matmul(TAILR, F1[:, P - 1:P], ident[0:BT, 0:BT], start=True, stop=True).then_inc(sm_t, 1)
                t.wait_ge(sm, b * 14 + 4)
                t.matmul(HEADR, Bh[:, 0:1], ident[0:BT, 0:BT], start=True, stop=True).then_inc(sm_t, 1)
                t.wait_ge(sm, b * 14 + 5)
                t.matmul(CINC, rowC[0:1, 0:BT], onesr[0:1, 0:1], start=True, stop=True).then_inc(sm_t, 1)
                t.wait_ge(sm, b * 14 + 7)
                t.matmul(CINK, rowK[0:1, :], onesr[0:1, 0:1], start=True, stop=True).then_inc(sm_t, 1)
                t.wait_ge(sm, b * 14 + 13)
                t.transpose(W_T, wr[:, :], ident[0:BT, 0:BT]).then_inc(sm_t, 1)
                t.wait_ge(sm, b * 14 + 14)
                t.matmul(FB, onesr[0:1, 0:C0], fr[0:1, 0:1], start=True, stop=True).then_inc(sm_t, 1)
                alone(t, exp_ready, b * 2 + 2)
                with t.Fori(0, BB // 2) as i:
                    for sl in range(2):
                        n = b * BB + i * 2 + sl
                        offs = offsets(n)
                        t.wait_ge(onehots, n + 1)
                        t.wait_ge(mp_free, n + 1)
                        add_batch(MPb[sl], C0, [SR[:, sl, j, :] for j in range(QT)], sl, offs).then_inc(agg, 1)

            with t.Fori(0, NCG // 2) as i:
                for k in range(2):
                    c7 = i * 2 + k
                    t.wait_ge(stg, 2 * (c7 + 1))
                    for j in range(CG):
                        mm = t.matmul(HP[k][:, j, :], accS[0:C0, j * P:(j + 1) * P], R0[:, :], start=True, stop=True)
                    mm.then_inc(hp_ready, 1)

            def batch1(n, i, s, tiles):
                offs = offsets(n)
                t.wait_ge(u1, n + 1)
                t.wait_ge(g1[s], i * QT * 16 + tiles * 16)
                t.wait_ge(at1[s], (i + 1) * 16)
                t.wait_ge(mp1_free, n + 1)
                add_batch(MPb[s % NS], C1, [ring[:, s * QT + j, :] for j in range(tiles)], s % NS, offs).then_inc(agg1, 1)

            def round1(i, self_term):
                for s in range(RG):
                    n = i * RG + s
                    if self_term and s == 1:
                        alone(t, xs_r, i + 1)
                        t.transpose(B[0][0:D, 0:NP], xs[:, :], ident[0:NP, 0:NP]).then_inc(xst_r, 1)
                    if self_term and s == 3:
                        t.wait_ge(xT_r, i + 1)
                        t.matmul(B[1][0:NP, 0:D], xT[:, :], SW[:, :], start=True, stop=True).then_inc(y_p, 1)
                    batch1(n, i, s, QT)

            t.wait_ge(sw_ready, 1)
            t.wait_ge(ring_ones, 1)
            with t.Fori(0, NJ) as i:
                round1(i, True)
            with t.Fori(NJ, R1N) as i:
                round1(i, False)
            batch1(R1N * RG, R1N, 0, QT)
            batch1(R1N * RG + 1, R1N, 1, 1)
            with t.Fori(0, NCG // 2) as i:
                for k in range(2):
                    c7 = i * 2 + k
                    t.wait_ge(stg1, 2 * (c7 + 1))
                    for j in range(CG):
                        mm = t.matmul(HQ[k][:, j, :], accS[0:C1, j * P:(j + 1) * P], R1[:, :], start=True, stop=True)
                    mm.then_inc(hq_ready, 1)

        @block.scalar
        def _(a):
            a.wait_ge(r0_ld, 32)
            a.wait_ge(tab0, 32)

            def evacuate(bank, cols, n, free):
                r = a.value_load(r0row[0:1, bass.ds(n, 1)], min_val=0, max_val=ACCW - WIN)
                alone(a, agg if cols == C0 else agg1, n + 1 + (2 if cols == C0 else RG))
                alone(a, free, n + 2)
                a.activation(acc[0:cols, bass.ds(r + 1, WIN - 1)], bank[0:cols, 1:WIN], ACT.Copy)
                a.activation(acc[0:cols, bass.ds(r, 1)], bank[0:cols, 0:1], ACT.Identity,
                             bias=acc[0:cols, bass.ds(r, 1)]).then_inc(free, 1)

            with a.Fori(0, NB) as b:
                with a.Fori(0, BB // 2) as i:
                    for sl in range(2):
                        n = b * BB + i * 2 + sl
                        a.wait_ge(hb_ready, n + 1)
                        a.wait_ge(onehot_hi, n + 1)
                        a.activation(HY[:, sl, :], HBb[sl][0:NHI, :], ACT.Abs, bias=nhi[0:NHI, 0:1]).then_inc(hb_used, 1)
                        a.wait_ge(hb_used, n + 3)
                        a.wait_ge(ed_ready, n + 1)
                        a.activation(OH[:, sl, :], HY[:, sl, :], ACT.Relu, scale=-1.0, bias=onesr[0:NHI, 0:1]).then_inc(onehot_hi, 1)
                r = a.value_load(r0row[0:1, bass.ds(b * BB, 1)], min_val=0, max_val=ACCW - WIN)
                a.wait_ge(sm_t, b * 7 + 6)
                a.activation(WD[:, :, 0], W_T, ACT.Exp).then_inc(exp_ready, 1)
                a.wait_ge(sm_t, b * 7 + 7)
                a.activation(Fs[:, :], FB, ACT.Exp, scale=fscale[:, 0:1]).then_inc(exp_ready, 1)
                alone(a, exp_ready, b * 2 + 2)
                alone(a, mp_free, b * BB + 2)
                a.activation(acc[0:C0, bass.ds(r, 1)], acc[0:C0, bass.ds(r, 1)], ACT.Identity,
                             scale=Fs[:, 0:1]).then_inc(rescaled, 1)
                alone(a, rescaled, b + 1)
                with a.Fori(0, BB // 2) as i:
                    for sl in range(2):
                        evacuate(MPb[sl], C0, b * BB + i * 2 + sl, mp_free)
            a.wait_ge(mp_free, NB * BB + 2)
            W = CG * P // 2
            with a.Fori(0, NCG) as c7:
                for h in range(2):
                    a.activation(accS[0:C0, h * W:(h + 1) * W], acc[0:C0, bass.ds(c7 * CG * P + h * W, W)], ACT.Copy).then_inc(stg, 1)
                a.wait_ge(hst_ready, c7 + 1)
            for c in range(NCH):
                a.wait_ge(ln, c * 7 + 5)
                a.activation(sd[:, :], var[:, :], ACT.Sqrt, scale=1.0 / D, bias=eps[0:NP, 0:1]).then_inc(ln_sd, 1)
            a.wait_ge(acc_zero1, 1)

            def round1(i, self_term):
                if self_term:
                    a.activation(xs[:, :], x1v[:, i, :], ACT.Copy).then_inc(xs_r, 1)
                for s in range(RG):
                    evacuate(MPb[s % NS], C1, i * RG + s, mp1_free)

            with a.Fori(0, NJ) as i:
                round1(i, True)
            with a.Fori(NJ, R1N) as i:
                round1(i, False)
            evacuate(MPb[0], C1, R1N * RG, mp1_free)
            evacuate(MPb[1], C1, R1N * RG + 1, mp1_free)
            a.wait_ge(mp1_free, R1N * RG + 4)
            with a.Fori(0, NCG) as c7:
                for h in range(2):
                    a.activation(accS[0:C1, h * W:(h + 1) * W], acc[0:C1, bass.ds(c7 * CG * P + h * W, W)], ACT.Copy).then_inc(stg1, 1)
                a.wait_ge(hst2_ready, c7 + 1)
            for c in range(NCH):
                a.wait_ge(ln2, c * 7 + 5)
                a.activation(sd[:, :], var[:, :], ACT.Sqrt, scale=1.0 / D, bias=eps[0:NP, 0:1]).then_inc(ln2_sd, 1)


_INS = ['x', 'src', 'dst', 'edge_attr_32', 'L0_gnn_fc_w', 'L0_gnn_attn_w', 'L1_gnn_msg_w', 'L1_gnn_msg_b',
        'L1_gnn_self_w', 'L1_gnn_self_b']


def kernel(**inputs):
    import numpy as _np
    import concourse.bacc as _bacc
    from concourse import mybir as _mybir
    from concourse.bass_utils import run_bass_kernel_spmd as _run

    nc = _bacc.Bacc("TRN2", target_bir_lowering=False, num_devices=1)
    arrays, args = {}, []
    for name in _INS:
        a = _np.ascontiguousarray(inputs[name])
        arrays[f"in_{name}_dram"] = a
        args.append(nc.dram_tensor(f"in_{name}_dram", a.shape, _mybir.dt.from_np(a.dtype), kind="ExternalInput").ap())
    args.append(nc.dram_tensor("out_0_dram", inputs['x'].shape, _mybir.dt.float32, kind="ExternalOutput").ap())
    gnn_layers(nc, *args)
    r = _run(nc, [arrays], core_ids=[0])
    return r.results[0]["out_0_dram"]
```

```python
import concourse.bass as bass
from concourse import mybir
from contextlib import ExitStack

ALU = mybir.AluOpType
ACT = mybir.ActivationFunctionType
AX = mybir.AxisListType
AX_X = AX.X
F32, BF16, I32 = mybir.dt.float32, mybir.dt.bfloat16, mybir.dt.int32

P = 128
BT = 112
GT = 16
QT = 4
WIN = QT * P
RG = 5
NEG = -1e38
SLOPE = 0.01
EPS = 1e-5


class Steps:

    def __init__(self, eng, sem, base=0):
        self.eng, self.sem, self.base, self.n = eng, sem, base, 0

    def did(self, ins):
        ins.then_inc(self.sem, 1)
        self.n += 1
        return self.n

    def wait(self, n=None):
        self.eng.wait_ge(self.sem, self.base + (self.n if n is None else n))


def gnn_layers(nc, x, src, dst, edge_attr, fc_w, attn_w, msg_w, msg_b, self_w, self_b, out):
    N, D = x.shape
    E = src.shape[0]
    DE = edge_attr.shape[1]
    NR = E // P
    NB = -(-NR // BT)
    NT = NB * BT
    LASTQ = NR - (NB - 1) * BT
    NG = BT // GT
    GB = GT // QT
    BB = BT // QT
    NHI = (N + P - 1) // P
    TAIL = N - (NHI - 1) * P
    RC = NHI
    CG = 7
    NCG = RC // CG
    ACCW = (RC + QT) * P
    NP = 125
    NJ = N // NP
    NCH = 4
    JC = NJ // NCH
    C0 = D + 2
    C1 = D + DE + 1
    R1N = NR // (RG * QT)
    NS = 3
    NCONST = 13
    assert NR * P == E and RC % CG == 0 and NP * NJ == N and D == 64
    assert R1N * RG * QT + QT + 1 == NR and BB % 2 == 0 and NB % 2 == 0 and NJ <= R1N
    assert (NCG * CG * P) <= ACCW and N + (NT - NR) + WIN <= ACCW

    h_dram = nc.dram_tensor("h_by_node", (N + P, D), F32).ap()
    a_dram = nc.dram_tensor("agg_by_node", (N + P, D), F32).ap()
    x1_dram = nc.dram_tensor("x1_by_node", (N, D), F32).ap()
    rec_dram = nc.dram_tensor("sorted_edges", (E, DE + 2), F32).ap()
    next_dram = nc.dram_tensor("next_place", (N + P, 1), F32).ap()
    r0_dram = nc.dram_tensor("first_rank", (NB, BB), I32).ap()
    d_dram = nc.dram_tensor("tile_offset", (NB, BT), I32).ap()

    def alone(eng, s, value):
        eng.wait_ge(s, value)
        eng.sem_inc(passed, 1)

    with ExitStack() as ctx:
        def sb(name, shape, dt=F32):
            return ctx.enter_context(nc.sbuf_tensor(name, shape, dt))

        def psum(name, shape):
            return ctx.enter_context(nc.psum_tensor(name, shape, F32))

        def sem(name):
            return ctx.enter_context(nc.semaphore(name))

        acc = sb("acc", [P, ACCW])
        G = sb("G", [P, 2 * BT * D])
        idx = sb("idx", [P, NT + BT], I32)
        idxg = sb("idxg", [P, 2, BT], I32)
        idg = sb("idg", [P, CG], I32)
        rel = sb("rel", [P, NT])
        dst_i = sb("dst_i", [BT, NB, P], I32)
        st = sb("st", [BT, NB, P], BF16)
        r0row = sb("r0row", [1, NB * BB], I32)
        drow = sb("drow", [1, NT], I32)
        prev_i = sb("prev_i", [BT, NB], I32)
        fall_q = sb("fall_q", [BT, 1])
        flag = sb("flag", [1, 1], I32)
        resets = sb("resets", [BT, NB, 3])
        pack3 = sb("pack3", [BT, 3])
        row3 = sb("row3", [1, 3, P])
        rowR = sb("rowR", [1, BT])
        inner = sb("inner", [BT, NB])
        cnt = sb("cnt", [BT, NB])
        st0 = sb("st0", [BT, NB])
        ident = sb("ident", [P, P])
        identb = sb("identb", [P, P], BF16)
        iota = sb("iota", [P, P])
        pidx = sb("pidx", [P, 1])
        dump = sb("dump", [P, 1])
        onesr = sb("onesr", [P, P])
        low = sb("low", [NB, NB])
        base0 = sb("base0", [NB, 1])
        r0i = sb("r0i", [NB, BT], I32)
        di = sb("di", [NB, BT], I32)
        srcf = sb("srcf", [BT, P])
        relrow = sb("relrow", [BT, P])
        fcw = sb("fcw", [D, D])
        acol = sb("acol", [D, 2])
        vsb = sb("vsb", [P, D])
        vdb = sb("vdb", [P, D])
        ED = sb("ED", [NHI, P])
        EDr = sb("EDr", [NHI, P])
        EDp = sb("EDp", [NHI, 3, P], BF16)
        R0 = sb("R0", [C0, C0])
        R1 = sb("R1", [C1, D + 1])
        SW = sb("SW", [D + 1, D])
        loi = sb("loi", [BT, P], I32)
        lof = sb("lof", [BT, P])
        hii = sb("hii", [BT, P], I32)
        hib = sb("hib", [BT, P], BF16)
        stdr = sb("stdr", [BT, P])
        negst = sb("negst", [BT, P + 1])
        loT = sb("loT", [P, BT])
        stT = sb("stT", [P, BT])
        WD = sb("WD", [P, BT, 2])
        HY = sb("HY", [NHI, 2, WIN], BF16)
        L0 = sb("L0", [P, 2 * QT * C0 + QT * (P + D) + 5 * P + 2 * BT])
        OH = sb("OH", [NHI, 2, WIN], BF16)
        nhi = sb("nhi", [P, 1])
        zrow = sb("zrow", [1, WIN], BF16)
        es = sb("es", [P, BT])
        ed = sb("ed", [P, BT])
        fr = sb("fr", [1, 1])
        Kin = sb("Kin", [BT, 1])
        rowH = sb("rowH", [1, BT + 1])
        rowK = sb("rowK", [1, BT])
        Cin = sb("Cin", [BT, 1])
        rowC = sb("rowC", [1, BT + 1])
        Fs = sb("Fs", [C0, 1])
        fscale = sb("fscale", [C0, 1])
        U = sb("U", [P, NS, QT, P])
        nz = sb("nz", [P, CG])
        den = sb("den", [P, CG])
        rcp = sb("rcp", [P, CG])
        idT = sb("idT", [P, RC], I32)
        mean = sb("mean", [NP, JC])
        var = sb("var", [NP, JC])
        sd = sb("sd", [NP, JC])
        rstd = sb("rstd", [NP, JC])
        eps = sb("eps", [P, 1])
        xs = sb("xs", [NP, D])
        xT = sb("xT", [D + 1, NP])

        HB = psum("HB", [P, 1024])
        EDP = psum("EDP", [P, 1024])
        MP = psum("MP", [P, 1536])
        PF = psum("PF", [P, 512])

        cT, sT, cum, tmp0 = [acc[0:NB, 11776 + k * BT:11776 + (k + 1) * BT] for k in range(4)]
        cut = [0]

        def part(parts, *shape):
            size = 1
            for k in shape:
                size *= k
            v = L0[0:parts, cut[0]:cut[0] + size]
            cut[0] += size
            if len(shape) == 2:
                v = v.rearrange("p (a b) -> p a b", a=shape[0])
            if len(shape) == 3:
                v = v.rearrange("p (a b c) -> p a b c", a=shape[0], b=shape[1])
            return v

        SR = part(P, 2, QT, C0)
        selj = part(P, QT, P)
        esx = part(P, QT, D)
        F1, F2, M, wr, Bh = [part(BT, P) for _ in range(5)]
        S0, S = part(P, BT), part(P, BT)
        ring = L0[:, 0:RG * QT * C1].rearrange("p (t c) -> p t c", c=C1)
        accS = U[:, :, :, :].rearrange("p s j r -> p (s j r)")[0:C1, 0:CG * P]
        Gt = G[:, :].rearrange("p (t d) -> p t d", d=D)
        src_i = acc[0:BT, 8192:8192 + NB * P].bitcast(I32).rearrange("q (b e) -> q b e", e=P)
        xhi = acc[0:NHI, 0:P * D]
        hst = G[:, 0:RC * D].rearrange("p (c d) -> p c d", d=D)
        ND = NJ * D
        x1v = G[0:NP, ND:2 * ND].rearrange("p (j d) -> p j d", d=D)
        yv = G[0:NP, 0:ND].rearrange("p (j d) -> p j d", d=D)
        hst2 = G[:, ND:ND + RC * D].rearrange("p (c d) -> p c d", d=D)
        hv = acc[0:NP, 0:ND].rearrange("p (j d) -> p j d", d=D)
        sqv = acc[0:NP, ND:ND + JC * D].rearrange("p (j d) -> p j d", d=D)
        MPb = [MP[:, 512 * k:512 * (k + 1)] for k in range(3)]
        B = [HB[:, 0:512], HB[:, 512:1024], EDP[:, 0:512], EDP[:, 512:1024], PF[:, :]]
        HBb = [B[0], B[1]]
        EDb = [B[k].rearrange("p (j r) -> p j r", r=P) for k in (2, 3)]
        LO_T, ID_T, ROWS = B[0][:, 0:BT], B[1][:, 0:BT], B[2][0:1, 0:3 * P].rearrange("o (k q) -> o k q", k=3)
        S_T, TAILR, HEADR, W_T = B[2][0:BT, 0:P], B[0][0:1, 0:BT], B[1][0:1, 0:BT], B[3][:, 0:BT]
        CINC, CINK, FB = B[0][0:BT, 0:1], B[1][0:BT, 0:1], B[4][0:C0, 0:1]
        HP = [HB[:, 0:CG * C0].rearrange("p (j c) -> p j c", c=C0),
              HB[:, 512:512 + CG * C0].rearrange("p (j c) -> p j c", c=C0)]
        HQ = [HB[:, 0:CG * (D + 1)].rearrange("p (j c) -> p j c", c=D + 1),
              HB[:, 512:512 + CG * (D + 1)].rearrange("p (j c) -> p j c", c=D + 1)]

        eye_d, same, below, sortj = [G[:, k * P:(k + 1) * P] for k in range(4)]
        rec = G[:, 512:512 + DE + 2]
        (dst_f, total, rank, place, now, new, last_f, gap, count0) = [G[:, 560 + k:561 + k] for k in range(9)]
        dst_c, place_i, keep_i = [G[:, 570 + k:571 + k].bitcast(I32) for k in range(3)]
        counts, upto, zeros_n = [G[0:NP, 600 + k * NJ:600 + (k + 1) * NJ] for k in range(3)]
        tri = G[0:NP, 1024:1024 + NP]

        falls, falls_sum, falls_ps, flag_ready = sem("falls"), sem("falls_sum"), sem("falls_ps"), sem("flag_ready")
        so_dst, so_dve, so_pe, so_got, so_kept = [[sem(f"{name}{k}") for k in range(2)]
                                                  for name in ("so_dst", "so_dve", "so_pe", "so_got", "so_kept")]
        so_rec, so_placed = [sem(f"so_rec{k}") for k in range(3)], sem("so_placed")
        so_set, so_zero, so_cnt, so_cntd, so_cntp, reload = (
            sem("so_set"), sem("so_zero"), sem("so_cnt"), sem("so_cntd"), sem("so_cntp"), sem("reload"))
        passed, rescaled = sem("passed"), sem("rescaled")
        idx_copied, id_copied, idx1_ready = sem("idx_copied"), sem("id_copied"), sem("idx1_ready")
        ld_edges, ld_prev, ld_w, ld_xhi = sem("ld_edges"), sem("ld_prev"), sem("ld_w"), sem("ld_xhi")
        prev_set, xhi_set, consts, consts2 = sem("prev_set"), sem("xhi_set"), sem("consts"), sem("consts2")
        pro, pro_t, idx_ready = sem("pro"), sem("pro_t"), sem("idx_ready")
        set_d, set_p, acc_zero, acc_zero1 = sem("set_d"), sem("set_p"), sem("acc_zero"), sem("acc_zero1")
        r0_done, r0_st, r0_ld, tab0 = sem("r0_done"), sem("r0_st"), sem("r0_ld"), sem("tab0")
        gathered = [sem(f"gathered{g}") for g in range(NG)]
        prep, prep_t = sem("prep"), sem("prep_t")
        pads, hb_used = sem("pads"), sem("hb_used")
        hb_ready, onehot_hi, ed_ready, ed_free, es_prod, es_ready = (
            sem("hb_ready"), sem("onehot_hi"), sem("ed_ready"), sem("ed_free"), sem("es_prod"), sem("es_ready"))
        sm, sm_t, exp_ready = sem("sm"), sem("sm_t"), sem("exp_ready")
        rows_scaled, onehots, agg, mp_free = sem("rows_scaled"), sem("onehots"), sem("agg"), sem("mp_free")
        stg, hp_ready, hp_used, hst_ready, scat = sem("stg"), sem("hp_ready"), sem("hp_used"), sem("hst_ready"), sem("scat")
        fin_d = sem("fin_d")
        ld_x, ld_h, ln, ln_sd, x1_ready, x1_st = sem("ld_x"), [sem(f"ld_h{c}") for c in range(NCH)], sem("ln"), sem("ln_sd"), sem("x1_ready"), sem("x1_st")
        ring_ones, sw_ready = sem("ring_ones"), sem("sw_ready")
        g1 = [sem(f"g1_{s}") for s in range(RG)]
        at1 = [sem(f"at1_{s}") for s in range(RG)]
        u1, agg1, mp1_free = sem("u1"), sem("agg1"), sem("mp1_free")
        xs_r, xst_r, xT_r, y_p, y_r = sem("xs_r"), sem("xst_r"), sem("xT_r"), sem("y_p"), sem("y_r")
        stg1, hq_ready, hq_used, hst2_ready, scat2, fin2 = (
            sem("stg1"), sem("hq_ready"), sem("hq_used"), sem("hst2_ready"), sem("scat2"), sem("fin2"))
        ld_a = [sem(f"ld_a{c}") for c in range(NCH)]
        ln2, ln2_sd, y_out, out_st = sem("ln2"), sem("ln2_sd"), sem("y_out"), sem("out_st")

        block = ctx.enter_context(nc.Block())

        def by_tile(e):
            n = (NB - 1) * BT * P
            return e[0:n].rearrange("(b q e) -> q b e", q=BT, e=P), e[n:E].rearrange("(q e) -> q e", e=P)

        at_given = edge_attr.rearrange("(t e) f -> e t f", e=P)
        at_sorted = rec_dram[:, 0:DE].rearrange("(t e) f -> e t f", e=P)

        def if_unsorted(eng):
            eng.wait_ge(flag_ready, 1)
            return eng.If(eng.value_load(flag[0:1, 0:1], min_val=0, max_val=1) > 0)

        def node_order(t):
            return t[0:N, :].rearrange("(p j) d -> p j d", p=NP)

        @block.sync
        def _(sp):
            with nc.allow_non_contiguous_dma(reason="one word per tile, and columns of weights"):
                sp.wait_ge(pads, 2)
                for t, e in ((src_i, src), (dst_i[:, :, :], dst)):
                    full, rest = by_tile(e)
                    sp.dma_start(t[:, 0:NB - 1, :], full).then_inc(ld_edges, 16)
                    sp.dma_start(t[0:LASTQ, NB - 1, :], rest).then_inc(ld_edges, 16)
                full, rest = by_tile(dst)
                sp.wait_ge(prev_set, 1)
                sp.dma_start(prev_i[1:BT, 0:NB - 1].unsqueeze(2), full[0:BT - 1, :, P - 1:P]).then_inc(ld_prev, 16)
                sp.dma_start(prev_i[0:1, 1:NB].unsqueeze(2), full[BT - 1:BT, :, P - 1:P]).then_inc(ld_prev, 16)
                sp.dma_start(prev_i[1:LASTQ, NB - 1:NB], rest[0:LASTQ - 1, P - 1:P]).then_inc(ld_prev, 16)
                sp.dma_start(fcw[:, :], fc_w).then_inc(ld_w, 16)
                sp.dma_start(acol[:, 0:1], attn_w[0, 0:D].unsqueeze(1)).then_inc(ld_w, 16)
                sp.dma_start(acol[:, 1:2], attn_w[0, D:2 * D].unsqueeze(1)).then_inc(ld_w, 16)
            with if_unsorted(sp):
                sp.wait_ge(so_set, 1)
                sp.dma_start(next_dram[0:N, 0].rearrange("(p j) -> p j", p=NP), zeros_n).then_inc(so_zero, 16)
                sp.dma_start(next_dram[N:N + P, :], count0).then_inc(so_zero, 16)
                sp.wait_ge(so_zero, 32)

                def load_edges(t, placing):
                    with nc.allow_non_contiguous_dma(reason="an edge on each partition"):
                        sp.dma_start(dst_c, dst[bass.ds(t * P, P)].unsqueeze(1)).then_inc(so_dst[placing], 16)
                        if placing:
                            sp.dma_start(rec[:, DE:DE + 1].bitcast(I32), src[bass.ds(t * P, P)].unsqueeze(1)).then_inc(so_rec[0], 16)
                            sp.dma_start(rec[:, DE + 1:DE + 2].bitcast(I32), dst[bass.ds(t * P, P)].unsqueeze(1)).then_inc(so_rec[1], 16)
                            sp.dma_start(rec[:, 0:DE], edge_attr[bass.ds(t * P, P), :]).then_inc(so_rec[2], 16)

                with sp.Fori(0, NR) as t:
                    load_edges(t, False)
                    alone(sp, so_kept[0], (t + 1) * 16)
                sp.dma_start(counts, next_dram[0:N, 0].rearrange("(p j) -> p j", p=NP)).then_inc(so_cnt, 16)
                sp.wait_ge(so_cntd, 3)
                sp.dma_start(next_dram[0:N, 0].rearrange("(p j) -> p j", p=NP), counts).then_inc(so_cnt, 16)
                sp.wait_ge(so_cnt, 32)
                with sp.Fori(0, NR) as t:
                    load_edges(t, True)
                    alone(sp, so_kept[1], (t + 1) * 16)
                    alone(sp, so_placed, (t + 1) * 16)
                with nc.allow_non_contiguous_dma(reason="one word of each record"):
                    by_edge = rec_dram.bitcast(I32)
                    for t, e in ((src_i, by_edge[:, DE]), (dst_i[:, :, :], by_edge[:, DE + 1])):
                        full, rest = by_tile(e)
                        for c in range(NB - 1):
                            sp.dma_start(t[:, c, :].unsqueeze(2), full[:, c, :].unsqueeze(2)).then_inc(reload, 16)
                        sp.dma_start(t[0:LASTQ, NB - 1, :].unsqueeze(2), rest.unsqueeze(2)).then_inc(reload, 16)
                    full, rest = by_tile(by_edge[:, DE + 1])
                    sp.dma_start(prev_i[1:BT, 0:NB - 1].unsqueeze(2), full[0:BT - 1, :, P - 1:P]).then_inc(reload, 16)
                    sp.dma_start(prev_i[0:1, 1:NB].unsqueeze(2), full[BT - 1:BT, :, P - 1:P]).then_inc(reload, 16)
                    sp.dma_start(prev_i[1:LASTQ, NB - 1:NB], rest[0:LASTQ - 1, P - 1:P]).then_inc(reload, 16)
                sp.wait_ge(reload, (2 * NB + 3) * 16)
            sp.wait_ge(xhi_set, 1)
            sp.dma_start(xhi[0:NHI - 1, :], x[0:(NHI - 1) * P, :].rearrange("(h l) d -> h (l d)", l=P)).then_inc(ld_xhi, 16)
            sp.dma_start(xhi[NHI - 1:NHI, 0:TAIL * D],
                         x[(NHI - 1) * P:N, :].rearrange("(h l) d -> h (l d)", h=1)).then_inc(ld_xhi, 16)
            sp.dma_start(R1[0:D + DE, 0:D], msg_w).then_inc(ld_w, 16)
            sp.dma_start(R1[D + DE:C1, 0:D], msg_b.unsqueeze(0)).then_inc(ld_w, 16)
            sp.dma_start(SW[0:D, :], self_w).then_inc(ld_w, 16)
            sp.dma_start(SW[D:D + 1, :], self_b.unsqueeze(0)).then_inc(ld_w, 16)
            sp.wait_ge(acc_zero, 1)
            for t in (h_dram, a_dram):
                sp.dma_start(node_order(t), hv).then_inc(tab0, 16)
            sp.wait_ge(r0_done, 1)
            with nc.allow_non_contiguous_dma(reason="first tile of each batch"):
                sp.dma_start(r0_dram.unsqueeze(2), r0i[:, :].rearrange("b (n j) -> b n j", j=QT)[:, :, 0:1]).then_inc(r0_st, 16)
            sp.dma_start(d_dram, di[:, :]).then_inc(r0_st, 16)
            sp.wait_ge(r0_st, 32)
            sp.dma_start(r0row[0:1, :], r0_dram.rearrange("b t -> (b t)").unsqueeze(0)).then_inc(r0_ld, 16)
            sp.dma_start(drow[0:1, :], d_dram.rearrange("b t -> (b t)").unsqueeze(0)).then_inc(r0_ld, 16)
            sp.wait_ge(rows_scaled, NB * BB + 2 * BB)
            sp.dma_start(x1v, node_order(x)).then_inc(ld_x, 16)
            sp.wait_ge(scat, RC * 16)
            sp.wait_ge(stg, 2 * NCG)
            for c in range(NCH):
                sp.dma_start(hv[:, c * JC:(c + 1) * JC, :],
                             node_order(h_dram)[:, c * JC:(c + 1) * JC, :]).then_inc(ld_h[c], 16)
            for c in range(NCH):
                sp.wait_ge(x1_ready, c + 1)
                sp.dma_start(node_order(x1_dram)[:, c * JC:(c + 1) * JC, :],
                             x1v[:, c * JC:(c + 1) * JC, :]).then_inc(x1_st, 16)
            def load_attrs(attr):
                def load_attr(n, s, tiles):
                    sp.wait_ge(agg1, n + 1)
                    sp.dma_start(ring[:, s * QT:s * QT + tiles, D:D + DE],
                                 attr[:, bass.ds(n * QT, tiles), :]).then_inc(at1[s], 16)

                with sp.Fori(0, R1N) as i:
                    for s in range(RG):
                        load_attr(i * RG + s, s, QT)
                load_attr(R1N * RG, 0, QT)
                load_attr(R1N * RG + 1, 1, 1)

            with if_unsorted(sp):
                load_attrs(at_sorted)
            with sp.Else():
                load_attrs(at_given)
            sp.wait_ge(scat2, RC * 16)
            sp.wait_ge(stg1, 2 * NCG)
            for c in range(NCH):
                sp.dma_start(hv[:, c * JC:(c + 1) * JC, :],
                             node_order(a_dram)[:, c * JC:(c + 1) * JC, :]).then_inc(ld_a[c], 16)
            for c in range(NCH):
                sp.wait_ge(y_out, c + 1)
                sp.dma_start(node_order(out)[:, c * JC:(c + 1) * JC, :],
                             yv[:, c * JC:(c + 1) * JC, :]).then_inc(out_st, 16)
            sp.wait_ge(out_st, NCH * 16)

        @block.gpsimd
        def _(g):
            c = Steps(g, consts)
            g.memset(src_i, 0).then_inc(pads, 1)
            g.wait_ge(pads, 1)
            g.memset(dst_i[:, :, :], -1).then_inc(pads, 1)
            g.wait_ge(pads, 2)
            g.memset(prev_i[:, :], -2).then_inc(prev_set, 1)
            g.wait_ge(prev_set, 1)
            g.memset(xhi[96:NHI, :], 0.0).then_inc(xhi_set, 1)
            g.wait_ge(xhi_set, 1)
            for tile, value in ((onesr, 1.0), (eps, EPS), (rowC, NEG), (rowH, NEG), (relrow, 0.0), (negst, 0.0), (fscale, 1.0),
                                (ident, 0.0)):
                c.did(g.memset(tile[:, :], value))
                c.wait()
            for tile, pattern, first, by_partition in ((iota, [[1, P]], 0, 0), (pidx, [[0, 1]], 0, 1), (dump, [[0, 1]], N, 1)):
                c.did(g.iota(tile[:, :], pattern=pattern, base=first, channel_multiplier=by_partition,
                             allow_small_or_imprecise_dtypes=True))
                c.wait()
            c.did(g.affine_select(out=ident[:, :], in_=ident[:, :], compare_op=ALU.not_equal, fill=1.0,
                                  base=0, pattern=[[-1, P]], channel_multiplier=1))
            c.wait()
            c.did(g.affine_select(out=fscale[:, :], in_=fscale[:, :], compare_op=ALU.not_equal, fill=0.0,
                                  base=-(D + 1), pattern=[[0, 1]], channel_multiplier=1))
            assert c.n == NCONST

            with if_unsorted(g):
                for placing in (False, True):
                    with g.Fori(0, NR) as t:
                        alone(g, so_dve[placing], t * 11 + 8)
                        g.indirect_dma_start(now, None, next_dram[:, :],
                                             bass.IndirectOffsetOnAxis(ap=dst_c, axis=0)).then_inc(so_got[placing], 16)
                        alone(g, so_dve[placing], t * 11 + 11)
                        if placing:
                            for q in so_rec:
                                alone(g, q, (t + 1) * 16)
                            g.indirect_dma_start(rec_dram[:, :], bass.IndirectOffsetOnAxis(ap=place_i, axis=0),
                                                 rec, None).then_inc(so_placed, 16)
                        g.indirect_dma_start(next_dram[:, :], bass.IndirectOffsetOnAxis(ap=keep_i, axis=0),
                                             new, None).then_inc(so_kept[placing], 16)
                        alone(g, so_kept[placing], (t + 1) * 16)
                        if placing:
                            alone(g, so_placed, (t + 1) * 16)

            def gather_block(b, half):
                alone(g, idx_copied, b + 1)
                for k in range(NG):
                    alone(g, rows_scaled, b * BB + (k + 1) * GB)
                    alone(g, es_ready, b * BB + (k + 1) * GB + 1)
                    for j in range(GT):
                        g.indirect_dma_start(Gt[:, half * BT + k * GT + j, :], None, x[:, :],
                                             bass.IndirectOffsetOnAxis(ap=idxg[:, half, k * GT + j:k * GT + j + 1], axis=0)
                                             ).then_inc(gathered[k], 16)

            with g.Fori(0, NB // 2) as b2:
                for half in range(2):
                    gather_block(b2 * 2 + half, half)

            g.wait_ge(tab0, 32)
            for c7 in range(NCG):
                g.wait_ge(hst_ready, c7 + 1)
                for j in range(c7 * CG, (c7 + 1) * CG):
                    g.indirect_dma_start(h_dram[:, :], bass.IndirectOffsetOnAxis(ap=idT[:, j:j + 1], axis=0),
                                         hst[:, j, :], None).then_inc(scat, 16)

            g.wait_ge(x1_st, NCH * 16)
            g.wait_ge(ring_ones, 1)
            def gather1(n, s, tiles):
                    alone(g, idx1_ready, n + 1)
                    for j in range(tiles):
                        g.indirect_dma_start(ring[:, s * QT + j, 0:D], None, x1_dram[:, :],
                                             bass.IndirectOffsetOnAxis(ap=idxg[:, 0, s * QT + j:s * QT + j + 1], axis=0)
                                             ).then_inc(g1[s], 16)

            with g.Fori(0, R1N) as i:
                for s in range(RG):
                    gather1(i * RG + s, s, QT)
            gather1(R1N * RG, 0, QT)
            gather1(R1N * RG + 1, 1, 1)

            for c7 in range(NCG):
                g.wait_ge(hst2_ready, c7 + 1)
                for j in range(c7 * CG, (c7 + 1) * CG):
                    g.indirect_dma_start(a_dram[:, :], bass.IndirectOffsetOnAxis(ap=idT[:, j:j + 1], axis=0),
                                         hst2[:, j, :], None).then_inc(scat2, 16)

        @block.vector
        def _(v):
            for free, buffers in ((es_ready, 1 + BB), (ed_free, 2), (rows_scaled, 2 * BB), (agg, 2), (agg1, RG),
                                  (mp_free, 2), (mp1_free, 2), (hb_used, 2), (onehot_hi, 2), (ed_ready, 2)):
                v.sem_inc(free, buffers)

            d = Steps(v, set_d)
            v.wait_ge(consts, NCONST)
            d.did(v.tensor_copy(identb[:, :], ident[:, :]))
            d.did(v.tensor_tensor(low[:, :], iota[0:NB, 0:NB], pidx[0:NB, 0:1].to_broadcast([NB, NB]), ALU.is_gt))
            v.memset(row3[:, :, :], 0.0)
            v.memset(zrow[:, :], 0.0)
            v.tensor_scalar(nhi[:, :], pidx[:, :], -1.0, None, ALU.mult)
            v.wait_ge(ld_edges, 64)
            v.wait_ge(ld_prev, 48)
            v.tensor_tensor(st[:, :, 1:P], dst_i[:, :, 1:P], dst_i[:, :, 0:P - 1], ALU.is_lt)
            v.tensor_tensor(st[:, :, 0:1], dst_i[:, :, 0:1], prev_i[:, :].unsqueeze(2), ALU.is_lt).then_inc(falls, 1)
            v.wait_ge(falls, 1)
            v.tensor_reduce(fall_q[:, :], st[:, :, :], AX.XY, ALU.add).then_inc(falls, 1)
            v.wait_ge(falls_ps, 1)
            v.tensor_scalar(flag[:, :], B[0][0:1, 0:1], 0.0, None, ALU.is_gt).then_inc(flag_ready, 1)
            with if_unsorted(v):
                v.memset(zeros_n, 0.0)
                v.memset(count0, 0.0)
                v.tensor_tensor(tri, iota[0:NP, 0:NP], pidx[0:NP, 0:1].to_broadcast([NP, NP]), ALU.is_gt)
                v.tensor_tensor(below, iota[:, :], pidx[:, 0:1].to_broadcast([P, P]), ALU.is_lt).then_inc(so_set, 1)
                v.wait_ge(so_set, 1)
                for placing in (False, True):
                    with v.Fori(0, NR) as t:
                        p = Steps(v, so_dve[placing], t * 11)
                        v.wait_ge(so_dst[placing], (t + 1) * 16)
                        p.did(v.tensor_copy(dst_f, dst_c))
                        p.wait()
                        p.did(v.tensor_scalar(eye_d, ident[:, :], dst_f, None, ALU.mult))
                        v.wait_ge(so_pe[placing], t + 1)
                        p.did(v.tensor_scalar(same, B[0][:, 0:P], dst_f, None, ALU.is_equal))
                        p.wait()
                        p.did(v.tensor_reduce(total, same, AX_X, ALU.add))
                        p.did(v.tensor_tensor(sortj, same, below, ALU.mult))
                        p.wait()
                        p.did(v.tensor_reduce(rank, sortj, AX_X, ALU.add))
                        p.wait()
                        p.did(v.tensor_tensor(gap, total, rank, ALU.subtract))
                        p.wait()
                        p.did(v.tensor_scalar(last_f, gap, 1.0, None, ALU.is_equal))
                        p.wait()
                        v.wait_ge(so_got[placing], (t + 1) * 16)
                        p.did(v.tensor_tensor(gap, dst_f, dump[:, :], ALU.subtract))
                        v.tensor_tensor(place_i, now, rank, ALU.add)
                        v.tensor_tensor(new, now, total, ALU.add)
                        p.wait()
                        p.did(v.tensor_tensor(gap, gap, last_f, ALU.mult))
                        p.wait()
                        p.did(v.tensor_tensor(keep_i, gap, dump[:, :], ALU.add))
                        v.wait_ge(so_kept[placing], (t + 1) * 16)
                        if placing:
                            alone(v, so_placed, (t + 1) * 16)
                    if not placing:
                        v.wait_ge(so_cnt, 16)
                        v.tensor_tensor_scan(upto, onesr[0:NP, 0:NJ], counts, 0.0, ALU.mult, ALU.add).then_inc(so_cntd, 1)
                        v.wait_ge(so_cntd, 1)
                        v.tensor_tensor(counts, upto, counts, ALU.subtract).then_inc(so_cntd, 1)
                        v.wait_ge(so_cntp, 1)
                        v.tensor_copy(count0[0:NP, :], B[1][0:NP, 0:1]).then_inc(so_cntp, 1)
                        v.wait_ge(so_cntp, 2)
                        v.wait_ge(so_cntd, 2)
                        v.tensor_scalar(counts, counts, count0[0:NP, :], None, ALU.add).then_inc(so_cntd, 1)
                v.wait_ge(reload, (2 * NB + 3) * 16)
            v.tensor_tensor(st[:, :, 1:P], dst_i[:, :, 1:P], dst_i[:, :, 0:P - 1], ALU.not_equal)
            v.tensor_tensor(st[:, :, 0:1], dst_i[:, :, 0:1], prev_i[:, :].unsqueeze(2), ALU.not_equal)
            d.did(v.tensor_tensor(st0[:, :].unsqueeze(2), dst_i[:, :, 0:1], prev_i[:, :].unsqueeze(2), ALU.not_equal))
            d.wait()
            v.memset(idx[:, NT:NT + BT], 0)

            def ranks_of_block(b):
                p = Steps(v, pro, b * 5)
                q = Steps(v, pro_t, b * 2)
                p.did(v.tensor_copy(srcf[:, :], src_i[:, b, :]))
                p.did(v.tensor_tensor_scan(relrow[:, 1:P], onesr[0:BT, 0:P - 1], st[:, b, 1:P], 0.0, ALU.mult, ALU.add))
                p.wait()
                p.did(v.tensor_tensor(cnt[:, bass.ds(b, 1)], relrow[:, P - 1:P], st0[:, bass.ds(b, 1)], ALU.add))
                q.wait(1)
                p.did(v.tensor_copy(idx[:, bass.ds(b * BT, BT)], B[0][:, 0:BT]))
                q.wait(2)
                p.did(v.tensor_copy(rel[:, bass.ds(b * BT, BT)], B[1][:, 0:BT]))
                p.wait()

            for b in range(2):
                ranks_of_block(b)
                v.tensor_copy(idxg[:, b, :], idx[:, b * BT:(b + 1) * BT]).then_inc(idx_copied, 1)
            with v.Fori(2, NB) as b:
                ranks_of_block(b)

            v.wait_ge(pro, NB * 5)
            v.memset(rel[:, NR:NT], -1.0)
            v.tensor_tensor(inner[:, :], cnt[:, :], st0[:, :], ALU.subtract)
            v.tensor_scalar(resets[:, :, 0], cnt[:, :], 0.0, NEG, ALU.is_gt, ALU.mult)
            d.did(v.tensor_scalar(resets[:, :, 2], st0[:, :], NEG, None, ALU.mult))
            d.wait()
            v.tensor_scalar(resets[:, :, 1], inner[:, :], 0.0, NEG, ALU.is_gt, ALU.mult)
            v.wait_ge(set_p, 2)
            v.tensor_copy(cT[:, :], B[0][0:NB, 0:BT])
            d.did(v.tensor_copy(sT[:, :], B[0][0:NB, 128:128 + BT]))
            d.wait()
            d.did(v.tensor_tensor_scan(cum[:, :], onesr[0:NB, 0:BT], cT[:, :], 0.0, ALU.mult, ALU.add))
            d.wait()
            d.did(v.tensor_tensor(tmp0[:, :], cum[:, :], cT[:, :], ALU.subtract))
            v.wait_ge(set_p, 3)
            d.did(v.tensor_copy(base0[:, :], B[1][0:NB, 0:1]))
            d.wait()
            d.did(v.tensor_tensor(cum[:, :], tmp0[:, :], sT[:, :], ALU.add))
            d.wait()
            v.tensor_scalar(r0i[:, :], cum[:, :], base0[:, 0:1], -1.0, ALU.add, ALU.add)
            cum3 = cum[:, :].rearrange("b (n j) -> b n j", j=QT)
            v.tensor_tensor(di[:, :].rearrange("b (n j) -> b n j", j=QT), cum3,
                            cum3[:, :, 0:1].to_broadcast([NB, BB, QT]), ALU.subtract).then_inc(r0_done, 1)

            v.wait_ge(set_p, 6)
            v.tensor_copy(vsb[:, :], B[2][:, 0:D])
            v.tensor_copy(R0[:, :], ident[0:C0, 0:C0])
            v.tensor_copy(R1[:, D:D + 1], ident[0:C1, C1 - 1:C1])
            d.did(v.tensor_copy(vdb[:, :], B[2][:, 128:128 + D]))
            d.wait()
            v.wait_ge(set_p, 6)
            v.tensor_copy(R0[0:D, 0:D], B[2][0:D, 256:256 + D])
            v.wait_ge(ld_xhi, 32)
            xh3 = xhi.rearrange("h (l d) -> h l d", d=D)
            d.did(v.tensor_tensor(xh3, xh3, vdb[0:NHI, :].unsqueeze(1).to_broadcast([NHI, P, D]), ALU.mult))
            d.wait()
            d.did(v.tensor_reduce(ED[:, :], xh3, AX_X, ALU.add))
            d.wait()
            d.did(v.tensor_copy(EDp[:, 0, :], ED[:, :]))
            d.wait()
            d.did(v.tensor_tensor(EDr[:, :], ED[:, :], EDp[:, 0, :], ALU.subtract))
            d.wait()
            d.did(v.tensor_copy(EDp[:, 1, :], EDr[:, :]))
            d.wait()
            d.did(v.tensor_tensor(ED[:, :], EDr[:, :], EDp[:, 1, :], ALU.subtract))
            d.wait()
            d.did(v.tensor_copy(EDp[:, 2, :], ED[:, :]))
            v.memset(acc[:, :], 0.0).then_inc(acc_zero, 1)

            def row_forms(b):
                p = Steps(v, prep, b * 11)
                p.did(v.tensor_scalar(loi[:, :], dst_i[:, b, :], P - 1, None, ALU.bitwise_and))
                p.did(v.tensor_scalar(hii[:, :], dst_i[:, b, :], 7, None, ALU.logical_shift_right))
                p.wait()
                p.did(v.tensor_copy(lof[:, :], loi[:, :]))
                p.did(v.tensor_copy(hib[:, :], hii[:, :]))
                p.did(v.tensor_tensor(stdr[:, :], dst_i[:, b, :], st[:, b, :], ALU.mult))
                p.did(v.tensor_scalar(negst[:, 0:P], st[:, b, :], NEG, None, ALU.mult))
                p.did(v.tensor_copy(pack3[:, :], resets[:, b, :]))
                v.wait_ge(prep_t, b * 3 + 1)
                p.did(v.tensor_copy(loT[:, :], LO_T))
                v.wait_ge(prep_t, b * 3 + 2)
                p.did(v.tensor_copy(stT[:, :], ID_T))
                v.wait_ge(prep_t, b * 3 + 3)
                p.did(v.tensor_copy(row3[:, :, 0:BT], ROWS[:, :, 0:BT]))
                p.wait()
                p.did(v.tensor_tensor(rowR[:, :], row3[:, 1, 0:BT], row3[:, 2, 1:BT + 1], ALU.add))
                alone(v, prep, b * 11 + 11)

            def scores(b, i, sl):
                n = b * BB + i
                q0 = i * QT

                def pick(j):
                    return v.scalar_tensor_tensor(out=selj[:, j, :], in0=iota[:, :], scalar=loT[:, bass.ds(q0 + j, 1)],
                                                  in1=EDb[sl][:, j, :], op0=ALU.is_equal, op1=ALU.mult,
                                                  accum_out=ed[:, bass.ds(q0 + j, 1)])

                v.wait_ge(es_ready, n + 1 + BB)
                v.tensor_tensor(esx[:, :, :], Gt[:, bass.ds((b % 2) * BT + q0, QT), :],
                                vsb[:, :].unsqueeze(1).to_broadcast([P, QT, D]), ALU.mult).then_inc(es_prod, 1)
                v.wait_ge(ed_free, n + 2)
                v.wait_ge(ed_ready, n + 3)
                pick(0)
                pick(1)
                v.wait_ge(es_prod, n + 1)
                v.tensor_reduce(es[:, bass.ds(q0, QT)], esx[:, :, :], AX_X, ALU.add).then_inc(es_ready, 1)
                pick(2)
                pick(3).then_inc(ed_free, 1)

            def weigh(b, i, sl):
                n = b * BB + i
                q0 = i * QT
                v.wait_ge(agg, n + 1)
                v.tensor_tensor(SR[:, sl, :, 0:D], Gt[:, bass.ds((b % 2) * BT + q0, QT), :],
                                WD[:, bass.ds(q0, QT), 0:1].to_broadcast([P, QT, D]), ALU.mult).then_inc(rows_scaled, 1)
                v.tensor_copy(SR[:, sl, :, D:C0], WD[:, bass.ds(q0, QT), :])
                v.tensor_tensor(U[:, sl, :, :], iota[:, :].unsqueeze(1).to_broadcast([P, QT, P]),
                                rel[:, bass.ds(b * BT + q0, QT)].unsqueeze(2).to_broadcast([P, QT, P]),
                                ALU.is_equal).then_inc(onehots, 1)

            def maxima(b):
                p = Steps(v, sm, b * 15)
                v.wait_ge(ed_free, (b + 1) * BB + 2)
                p.did(v.tensor_tensor(S0[:, :], es[:, :], ed[:, :], ALU.add))
                p.wait()
                p.did(v.scalar_tensor_tensor(out=S[:, :], in0=S0[:, :], scalar=SLOPE, in1=S0[:, :],
                                             op0=ALU.mult, op1=ALU.max))
                v.wait_ge(sm_t, b * 7 + 1)
                p.did(v.tensor_tensor_scan(F1[:, :], negst[:, 0:P], S_T, NEG, ALU.add, ALU.max))
                p.did(v.tensor_tensor_scan(Bh[:, P - 1::-1], negst[:, P:0:-1], S_T[:, P - 1::-1], NEG, ALU.add, ALU.max))
                v.wait_ge(sm_t, b * 7 + 2)
                p.did(v.tensor_tensor_scan(rowC[0:1, 1:BT + 1], row3[:, 0, 0:BT], TAILR, rowC[0:1, 0:1], ALU.add, ALU.max))
                v.wait_ge(sm_t, b * 7 + 3)
                p.did(v.tensor_tensor_scan(rowH[0:1, BT - 1::-1], rowR[:, BT - 1::-1], HEADR[:, BT - 1::-1], NEG, ALU.add, ALU.max))
                p.wait()
                p.did(v.tensor_tensor(rowK[:, :], rowH[0:1, 1:BT + 1], row3[:, 2, 1:BT + 1], ALU.add))
                v.wait_ge(sm_t, b * 7 + 4)
                p.did(v.tensor_copy(Cin[:, :], CINC))
                v.wait_ge(sm_t, b * 7 + 5)
                p.did(v.tensor_copy(Kin[:, :], CINK))
                p.did(v.tensor_copy(rowC[0:1, 0:1], rowC[0:1, BT:BT + 1]))
                p.wait(9)
                p.did(v.tensor_tensor_scan(F2[:, :], negst[:, 0:P], S_T, Cin[:, 0:1], ALU.add, ALU.max))
                p.wait()
                p.did(v.tensor_tensor_scan(M[:, P - 1::-1], negst[:, P:0:-1], F2[:, P - 1::-1], Kin[:, 0:1], ALU.add, ALU.max))
                p.wait()
                p.did(v.tensor_tensor(wr[:, :], S_T, M[:, :], ALU.subtract))
                p.did(v.tensor_scalar(fr[:, :], Cin[0:1, :], M[0:1, 0:1], 0.0, ALU.subtract, ALU.min))
                v.wait_ge(agg, b * BB + 2)
                p.did(v.tensor_copy(WD[:, :, 1], stT[:, :]))
                alone(v, exp_ready, b * 2 + 1)
                alone(v, sm, b * 15 + 15)

            row_forms(0)
            for k in range(NG):
                v.wait_ge(gathered[k], GT * 16)
                with v.Fori(0, GB // 2) as i:
                    for sl in range(2):
                        scores(0, k * GB + i * 2 + sl, sl)
            maxima(0)
            with v.Fori(0, NB - 1) as b:
                row_forms(b + 1)
                v.tensor_copy(idxg[:, bass.ds(b % 2, 1), :], idx[:, bass.ds((b + 2) * BT, BT)].unsqueeze(1)).then_inc(idx_copied, 1)
                weigh(b, 0, 0)
                for k in range(NG):
                    alone(v, gathered[k], (b + 2) * GT * 16)
                    if k < NG - 1:
                        with v.Fori(0, GB // 2) as i:
                            for sl in range(2):
                                weigh(b, k * GB + i * 2 + sl + 1, 1 - sl)
                                scores(b + 1, k * GB + i * 2 + sl, sl)
                    else:
                        for i in range(k * GB, BB):
                            if i < BB - 1:
                                weigh(b, i + 1, 1 - i % 2)
                            scores(b + 1, i, i % 2)
                maxima(b + 1)
            with v.Fori(0, BB // 2) as i:
                for sl in range(2):
                    weigh(NB - 1, i * 2 + sl, sl)

            with v.Fori(0, NCG // 2) as i:
                for k in range(2):
                    c7 = i * 2 + k
                    f = Steps(v, fin_d, c7 * 4)
                    v.wait_ge(hp_ready, c7 + 1)
                    f.did(v.tensor_scalar(nz[:, :], HP[k][:, :, D], 0.0, None, ALU.is_equal))
                    f.wait()
                    f.did(v.tensor_tensor(den[:, :], HP[k][:, :, D], nz[:, :], ALU.add))
                    f.wait()
                    f.did(v.reciprocal(rcp[:, :], den[:, :]))
                    f.did(v.scalar_tensor_tensor(out=idT[:, bass.ds(c7 * CG, CG)], in0=nz[:, :], scalar=dump[:, 0:1],
                                                 in1=HP[k][:, :, D + 1], op0=ALU.mult, op1=ALU.add))
                    f.wait()
                    v.tensor_tensor(hst[:, bass.ds(c7 * CG, CG), :], HP[k][:, :, 0:D],
                                    rcp[:, :].unsqueeze(2).to_broadcast([P, CG, D]), ALU.mult).then_inc(hst_ready, 1)

            def layer_norm(a, r, c, s, s_sd, done):
                ac, rc = a[:, c * JC:(c + 1) * JC, :], r[:, c * JC:(c + 1) * JC, :]
                f = Steps(v, s, c * 7)
                f.did(v.tensor_tensor(ac, ac, rc, ALU.add))
                f.wait()
                f.did(v.tensor_reduce(mean[:, :], ac, AX_X, ALU.add))
                f.wait()
                f.did(v.scalar_tensor_tensor(out=ac, in0=mean[:, :].unsqueeze(2).to_broadcast([NP, JC, D]),
                                             scalar=-1.0 / D, in1=ac, op0=ALU.mult, op1=ALU.add))
                f.wait()
                f.did(v.tensor_tensor(sqv, ac, ac, ALU.mult))
                f.wait()
                f.did(v.tensor_reduce(var[:, :], sqv, AX_X, ALU.add))
                v.wait_ge(s_sd, c + 1)
                f.did(v.reciprocal(rstd[:, :], sd[:, :]))
                f.wait()
                f.did(v.tensor_tensor(ac, ac, rstd[:, :].unsqueeze(2).to_broadcast([NP, JC, D]), ALU.mult))
                f.wait()
                v.sem_inc(done, 1)

            v.wait_ge(ld_x, 16)
            for c in range(NCH):
                v.wait_ge(ld_h[c], 16)
                layer_norm(x1v, hv, c, ln, ln_sd, x1_ready)
            v.memset(ring[:, :, D + DE:C1], 1.0).then_inc(ring_ones, 1)
            v.memset(xT[D:D + 1, :], 1.0).then_inc(sw_ready, 1)
            v.memset(acc[:, :], 0.0).then_inc(acc_zero1, 1)

            def onehots1(n, s, tiles):
                v.wait_ge(agg1, n + 1)
                v.tensor_copy(idxg[:, 0, s * QT:s * QT + tiles], idx[:, bass.ds(n * QT, tiles)]).then_inc(idx1_ready, 1)
                v.wait_ge(agg1, n + RG - 1)
                v.tensor_tensor(U[:, s % NS, 0:tiles, :], iota[:, :].unsqueeze(1).to_broadcast([P, tiles, P]),
                                rel[:, bass.ds(n * QT, tiles)].unsqueeze(2).to_broadcast([P, tiles, P]),
                                ALU.is_equal).then_inc(u1, 1)

            def round1(i, self_term):
                for s in range(RG):
                    onehots1(i * RG + s, s, QT)
                    if self_term and s == 1:
                        v.wait_ge(xst_r, i + 1)
                        v.tensor_copy(xT[0:D, :], B[0][0:D, 0:NP]).then_inc(xT_r, 1)
                    if self_term and s == 3:
                        v.wait_ge(y_p, i + 1)
                        v.tensor_tensor(yv[:, i, :], B[1][0:NP, 0:D], x1v[:, i, :], ALU.add).then_inc(y_r, 1)

            with v.Fori(0, NJ) as i:
                round1(i, True)
            with v.Fori(NJ, R1N) as i:
                round1(i, False)
            onehots1(R1N * RG, 0, QT)
            onehots1(R1N * RG + 1, 1, 1)

            v.wait_ge(y_r, NJ)
            with v.Fori(0, NCG // 2) as i:
                for k in range(2):
                    c7 = i * 2 + k
                    f = Steps(v, fin2, c7 * 2)
                    v.wait_ge(hq_ready, c7 + 1)
                    f.did(v.tensor_scalar(den[:, :], HQ[k][:, :, D], 1.0, None, ALU.max))
                    f.wait()
                    f.did(v.reciprocal(rcp[:, :], den[:, :]))
                    f.wait()
                    v.tensor_tensor(hst2[:, bass.ds(c7 * CG, CG), :], HQ[k][:, :, 0:D],
                                    rcp[:, :].unsqueeze(2).to_broadcast([P, CG, D]), ALU.mult).then_inc(hst2_ready, 1)
            for c in range(NCH):
                v.wait_ge(ld_a[c], 16)
                layer_norm(yv, hv, c, ln2, ln2_sd, y_out)

        @block.tensor
        def _(t):
            def offsets(n):
                _, values = nc.values_load_multi_w_load_instructions(
                    drow[0:1, bass.ds(n * QT, QT)], engines=(mybir.EngineType.PE,), min_val=0, max_val=WIN - P)
                return values

            def add_batch(bank, cols, rows, sl, offs):
                t.matmul(bank[0:cols, :], zrow[0:1, 0:cols], zrow[0:1, :], start=True, stop=False, skip_group_check=True)
                for j, r in enumerate(rows):
                    mm = t.matmul(bank[0:cols, bass.ds(offs[j], P)], r, U[:, sl, j, :], start=False,
                                  stop=(j == len(rows) - 1), skip_group_check=True)
                return mm

            t.wait_ge(consts, NCONST)
            t.wait_ge(falls, 2)
            t.matmul(B[0][0:1, 0:1], fall_q[:, :], onesr[0:BT, 0:1], start=True, stop=True).then_inc(falls_ps, 1)
            with if_unsorted(t):
                for placing in (False, True):
                    with t.Fori(0, NR) as n:
                        t.wait_ge(so_dve[placing], n * 11 + 2)
                        t.matmul(B[0][:, 0:P], onesr[:, :], eye_d, start=True, stop=True).then_inc(so_pe[placing], 1)
                    if not placing:
                        t.wait_ge(so_cntd, 1)
                        t.matmul(B[1][0:NP, 0:1], tri, upto[:, NJ - 1:NJ], start=True, stop=True).then_inc(so_cntp, 1)
            with t.Fori(0, NB) as b:
                t.wait_ge(pro, b * 5 + 1)
                t.transpose(B[0][:, 0:BT], srcf[:, :], ident[0:BT, 0:BT]).then_inc(pro_t, 1)
                t.wait_ge(pro, b * 5 + 2)
                t.transpose(B[1][:, 0:BT], relrow[:, :], ident[0:BT, 0:BT]).then_inc(pro_t, 1)
            t.wait_ge(pro, NB * 5)
            t.wait_ge(set_d, 3)
            t.transpose(B[0][0:NB, 0:BT], cnt[:, :], ident[0:BT, 0:BT]).then_inc(set_p, 1)
            t.transpose(B[0][0:NB, 128:128 + BT], st0[:, :], ident[0:BT, 0:BT]).then_inc(set_p, 1)
            t.wait_ge(set_d, 6)
            t.matmul(B[1][0:NB, 0:1], low[:, :], cum[:, BT - 1:BT], start=True, stop=True).then_inc(set_p, 1)
            t.wait_ge(ld_w, 7 * 16)
            t.matmul(B[2][:, 0:D], acol[:, 0:1].to_broadcast([D, P]), fcw[:, :], start=True, stop=True).then_inc(set_p, 1)
            t.matmul(B[2][:, 128:128 + D], acol[:, 1:2].to_broadcast([D, P]), fcw[:, :], start=True, stop=True).then_inc(set_p, 1)
            t.transpose(B[2][0:D, 256:256 + D], fcw[:, :], ident[0:D, 0:D]).then_inc(set_p, 1)

            t.wait_ge(acc_zero, 1)
            t.wait_ge(r0_ld, 32)
            def row_forms(b):
                t.wait_ge(prep, b * 11 + 7)
                t.transpose(LO_T, lof[:, :], ident[0:BT, 0:BT]).then_inc(prep_t, 1)
                t.transpose(ID_T, stdr[:, :], ident[0:BT, 0:BT]).then_inc(prep_t, 1)
                for k in range(3):
                    mm = t.matmul(ROWS[:, k, 0:BT], pack3[:, k:k + 1], ident[0:BT, 0:BT], start=True, stop=True)
                mm.then_inc(prep_t, 1)
                alone(t, prep, b * 11 + 10)

            def spread_hi(b, i, sl):
                t.wait_ge(hb_used, b * BB + i + 1)
                for j in range(QT):
                    mm = t.matmul(HBb[sl][0:NHI, j * P:(j + 1) * P],
                                  identb[0:BT, bass.ds(i * QT + j, 1)].to_broadcast([BT, NHI]),
                                  hib[:, :], start=True, stop=True)
                mm.then_inc(hb_ready, 1)

            def choose_hi(b, i, sl):
                n = b * BB + i
                t.wait_ge(onehot_hi, n + 3)
                t.wait_ge(ed_free, n + 1)
                for j in range(QT):
                    for c in range(3):
                        mm = t.matmul(EDb[sl][:, j, :], OH[:, sl, j * P:(j + 1) * P], EDp[:, c, :],
                                      start=(c == 0), stop=(c == 2))
                mm.then_inc(ed_ready, 1)

            def sum_batch(b, i, sl):
                n = b * BB + i
                offs = offsets(n)
                t.wait_ge(onehots, n + 1)
                t.wait_ge(mp_free, n + 1)
                add_batch(MPb[sl], C0, [SR[:, sl, j, :] for j in range(QT)], sl, offs).then_inc(agg, 1)

            def maxima(b):
                t.wait_ge(sm, b * 15 + 2)
                t.transpose(S_T, S[:, :], ident[:, :]).then_inc(sm_t, 1)
                t.wait_ge(sm, b * 15 + 3)
                t.matmul(TAILR, F1[:, P - 1:P], ident[0:BT, 0:BT], start=True, stop=True).then_inc(sm_t, 1)
                t.wait_ge(sm, b * 15 + 4)
                t.matmul(HEADR, Bh[:, 0:1], ident[0:BT, 0:BT], start=True, stop=True).then_inc(sm_t, 1)
                t.wait_ge(sm, b * 15 + 5)
                t.matmul(CINC, rowC[0:1, 0:BT], onesr[0:1, 0:1], start=True, stop=True).then_inc(sm_t, 1)
                t.wait_ge(sm, b * 15 + 7)
                t.matmul(CINK, rowK[0:1, :], onesr[0:1, 0:1], start=True, stop=True).then_inc(sm_t, 1)
                t.wait_ge(sm, b * 15 + 13)
                t.transpose(W_T, wr[:, :], ident[0:BT, 0:BT]).then_inc(sm_t, 1)
                t.wait_ge(sm, b * 15 + 14)
                t.matmul(FB, onesr[0:1, 0:C0], fr[0:1, 0:1], start=True, stop=True).then_inc(sm_t, 1)
                alone(t, exp_ready, b * 2 + 2)

            row_forms(0)
            spread_hi(0, 0, 0)
            with t.Fori(0, BB // 2 - 1) as i:
                for sl in range(2):
                    spread_hi(0, i * 2 + sl + 1, 1 - sl)
                    choose_hi(0, i * 2 + sl, sl)
            spread_hi(0, BB - 1, 1)
            choose_hi(0, BB - 2, 0)
            choose_hi(0, BB - 1, 1)
            maxima(0)
            with t.Fori(0, NB - 1) as b:
                row_forms(b + 1)
                spread_hi(b + 1, 0, 0)
                with t.Fori(0, BB // 2 - 1) as i:
                    for sl in range(2):
                        spread_hi(b + 1, i * 2 + sl + 1, 1 - sl)
                        sum_batch(b, i * 2 + sl, sl)
                        choose_hi(b + 1, i * 2 + sl, sl)
                spread_hi(b + 1, BB - 1, 1)
                for i in (BB - 2, BB - 1):
                    sum_batch(b, i, i % 2)
                    choose_hi(b + 1, i, i % 2)
                maxima(b + 1)
            with t.Fori(0, BB // 2) as i:
                for sl in range(2):
                    sum_batch(NB - 1, i * 2 + sl, sl)

            with t.Fori(0, NCG // 2) as i:
                for k in range(2):
                    c7 = i * 2 + k
                    t.wait_ge(stg, 2 * (c7 + 1))
                    for j in range(CG):
                        mm = t.matmul(HP[k][:, j, :], accS[0:C0, j * P:(j + 1) * P], R0[:, :], start=True, stop=True)
                    mm.then_inc(hp_ready, 1)

            def batch1(n, i, s, tiles):
                offs = offsets(n)
                t.wait_ge(u1, n + 1)
                t.wait_ge(g1[s], i * QT * 16 + tiles * 16)
                t.wait_ge(at1[s], (i + 1) * 16)
                t.wait_ge(mp1_free, n + 1)
                add_batch(MPb[s % NS], C1, [ring[:, s * QT + j, :] for j in range(tiles)], s % NS, offs).then_inc(agg1, 1)

            def round1(i, self_term):
                for s in range(RG):
                    n = i * RG + s
                    if self_term and s == 1:
                        alone(t, xs_r, i + 1)
                        t.transpose(B[0][0:D, 0:NP], xs[:, :], ident[0:NP, 0:NP]).then_inc(xst_r, 1)
                    if self_term and s == 3:
                        t.wait_ge(xT_r, i + 1)
                        t.matmul(B[1][0:NP, 0:D], xT[:, :], SW[:, :], start=True, stop=True).then_inc(y_p, 1)
                    batch1(n, i, s, QT)

            t.wait_ge(sw_ready, 1)
            t.wait_ge(ring_ones, 1)
            with t.Fori(0, NJ) as i:
                round1(i, True)
            with t.Fori(NJ, R1N) as i:
                round1(i, False)
            batch1(R1N * RG, R1N, 0, QT)
            batch1(R1N * RG + 1, R1N, 1, 1)
            with t.Fori(0, NCG // 2) as i:
                for k in range(2):
                    c7 = i * 2 + k
                    t.wait_ge(stg1, 2 * (c7 + 1))
                    for j in range(CG):
                        mm = t.matmul(HQ[k][:, j, :], accS[0:C1, j * P:(j + 1) * P], R1[:, :], start=True, stop=True)
                    mm.then_inc(hq_ready, 1)

        @block.scalar
        def _(a):
            a.wait_ge(r0_ld, 32)
            a.wait_ge(tab0, 32)

            def evacuate(bank, cols, n, free):
                r = a.value_load(r0row[0:1, bass.ds(n, 1)], min_val=0, max_val=ACCW - WIN)
                alone(a, agg if cols == C0 else agg1, n + 1 + (2 if cols == C0 else RG))
                alone(a, free, n + 2)
                a.activation(acc[0:cols, bass.ds(r + 1, WIN - 1)], bank[0:cols, 1:WIN], ACT.Copy)
                a.activation(acc[0:cols, bass.ds(r, 1)], bank[0:cols, 0:1], ACT.Identity,
                             bias=acc[0:cols, bass.ds(r, 1)]).then_inc(free, 1)

            def onehot_of_hi(b, i, sl):
                n = b * BB + i
                a.wait_ge(hb_ready, n + 1)
                a.wait_ge(onehot_hi, n + 1)
                a.activation(HY[:, sl, :], HBb[sl][0:NHI, :], ACT.Abs, bias=nhi[0:NHI, 0:1]).then_inc(hb_used, 1)
                a.wait_ge(hb_used, n + 3)
                a.wait_ge(ed_ready, n + 1)
                a.activation(OH[:, sl, :], HY[:, sl, :], ACT.Relu, scale=-1.0, bias=onesr[0:NHI, 0:1]).then_inc(onehot_hi, 1)

            def weights(b):
                r = a.value_load(r0row[0:1, bass.ds(b * BB, 1)], min_val=0, max_val=ACCW - WIN)
                a.wait_ge(sm_t, b * 7 + 6)
                alone(a, sm, b * 15 + 15)
                a.activation(WD[:, :, 0], W_T, ACT.Exp).then_inc(exp_ready, 1)
                a.wait_ge(sm_t, b * 7 + 7)
                a.activation(Fs[:, :], FB, ACT.Exp, scale=fscale[:, 0:1]).then_inc(exp_ready, 1)
                alone(a, exp_ready, b * 2 + 2)
                alone(a, mp_free, b * BB + 2)
                a.activation(acc[0:C0, bass.ds(r, 1)], acc[0:C0, bass.ds(r, 1)], ACT.Identity,
                             scale=Fs[:, 0:1]).then_inc(rescaled, 1)
                alone(a, rescaled, b + 1)

            with a.Fori(0, BB // 2) as i:
                for sl in range(2):
                    onehot_of_hi(0, i * 2 + sl, sl)
            weights(0)
            with a.Fori(0, NB - 1) as b:
                with a.Fori(0, BB // 2) as i:
                    for sl in range(2):
                        onehot_of_hi(b + 1, i * 2 + sl, sl)
                        evacuate(MPb[sl], C0, b * BB + i * 2 + sl, mp_free)
                weights(b + 1)
            with a.Fori(0, BB // 2) as i:
                for sl in range(2):
                    evacuate(MPb[sl], C0, (NB - 1) * BB + i * 2 + sl, mp_free)
            a.wait_ge(mp_free, NB * BB + 2)
            W = CG * P // 2
            with a.Fori(0, NCG) as c7:
                for h in range(2):
                    a.activation(accS[0:C0, h * W:(h + 1) * W], acc[0:C0, bass.ds(c7 * CG * P + h * W, W)], ACT.Copy).then_inc(stg, 1)
                a.wait_ge(hst_ready, c7 + 1)
            for c in range(NCH):
                a.wait_ge(ln, c * 7 + 5)
                a.activation(sd[:, :], var[:, :], ACT.Sqrt, scale=1.0 / D, bias=eps[0:NP, 0:1]).then_inc(ln_sd, 1)
            a.wait_ge(acc_zero1, 1)

            def round1(i, self_term):
                if self_term:
                    a.activation(xs[:, :], x1v[:, i, :], ACT.Copy).then_inc(xs_r, 1)
                for s in range(RG):
                    evacuate(MPb[s % NS], C1, i * RG + s, mp1_free)

            with a.Fori(0, NJ) as i:
                round1(i, True)
            with a.Fori(NJ, R1N) as i:
                round1(i, False)
            evacuate(MPb[0], C1, R1N * RG, mp1_free)
            evacuate(MPb[1], C1, R1N * RG + 1, mp1_free)
            a.wait_ge(mp1_free, R1N * RG + 4)
            with a.Fori(0, NCG) as c7:
                for h in range(2):
                    a.activation(accS[0:C1, h * W:(h + 1) * W], acc[0:C1, bass.ds(c7 * CG * P + h * W, W)], ACT.Copy).then_inc(stg1, 1)
                a.wait_ge(hst2_ready, c7 + 1)
            for c in range(NCH):
                a.wait_ge(ln2, c * 7 + 5)
                a.activation(sd[:, :], var[:, :], ACT.Sqrt, scale=1.0 / D, bias=eps[0:NP, 0:1]).then_inc(ln2_sd, 1)


_INS = ['x', 'src', 'dst', 'edge_attr_32', 'L0_gnn_fc_w', 'L0_gnn_attn_w', 'L1_gnn_msg_w', 'L1_gnn_msg_b',
        'L1_gnn_self_w', 'L1_gnn_self_b']


def kernel(**inputs):
    import numpy as _np
    import concourse.bacc as _bacc
    from concourse import mybir as _mybir
    from concourse.bass_utils import run_bass_kernel_spmd as _run

    nc = _bacc.Bacc("TRN2", target_bir_lowering=False, num_devices=1)
    arrays, args = {}, []
    for name in _INS:
        a = _np.ascontiguousarray(inputs[name])
        arrays[f"in_{name}_dram"] = a
        args.append(nc.dram_tensor(f"in_{name}_dram", a.shape, _mybir.dt.from_np(a.dtype), kind="ExternalInput").ap())
    args.append(nc.dram_tensor("out_0_dram", inputs['x'].shape, _mybir.dt.float32, kind="ExternalOutput").ap())
    gnn_layers(nc, *args)
    r = _run(nc, [arrays], core_ids=[0])
    return r.results[0]["out_0_dram"]
```

```python
import concourse.bass as bass
from concourse import mybir
from contextlib import ExitStack

ALU = mybir.AluOpType
ACT = mybir.ActivationFunctionType
AX = mybir.AxisListType
AX_X = AX.X
F32, BF16, I32 = mybir.dt.float32, mybir.dt.bfloat16, mybir.dt.int32

P = 128
BT = 112
GT = 16
QT = 4
WIN = QT * P
RG = 12
NEG = -1e38
SLOPE = 0.01
EPS = 1e-5


class Steps:

    def __init__(self, eng, sem, base=0):
        self.eng, self.sem, self.base, self.n = eng, sem, base, 0

    def did(self, ins):
        ins.then_inc(self.sem, 1)
        self.n += 1
        return self.n

    def wait(self, n=None):
        self.eng.wait_ge(self.sem, self.base + (self.n if n is None else n))


def gnn_layers(nc, x, src, dst, edge_attr, fc_w, attn_w, msg_w, msg_b, self_w, self_b, out):
    N, D = x.shape
    E = src.shape[0]
    DE = edge_attr.shape[1]
    NR = E // P
    NB = -(-NR // BT)
    NT = NB * BT
    LASTQ = NR - (NB - 1) * BT
    EMPTY = LASTQ // 32 * 32
    NG = BT // GT
    GB = GT // QT
    BB = BT // QT
    NHI = (N + P - 1) // P
    TAIL = N - (NHI - 1) * P
    RC = NHI
    CG = 7
    NCG = RC // CG
    ACCW = (RC + QT) * P
    NP = 125
    NJ = N // NP
    C0 = D + 2
    C1 = D + DE + 1
    R1N = NR // (RG * QT)
    HG = RG // 2
    NS = 3
    EG = 4
    EARLY = [(52, (0, EG)), (56, (EG, 2 * EG)), (62, (2 * EG, 3 * EG))]
    LAST_EARLY = len(EARLY) * EG
    NCONST = 14
    assert NR * P == E and RC % CG == 0 and NP * NJ == N and D == 64
    assert R1N * RG * QT + QT + 1 == NR and BB % 2 == 0 and NB % 2 == 0 and RC % 2 == 0 and RC <= 2 * R1N
    assert EARLY[0][0] > RC // 2 and EARLY[-1][0] < R1N - 2 and LAST_EARLY < NCG
    assert HG % NS == 0 and RG * QT * C1 <= BT * D and HG * QT <= BT
    assert NCG % 2 == 0 and RG * QT * C1 + 4 * CG * D <= BT * D and N - 1 + WIN < ACCW and BT - LASTQ < GT
    assert (NCG * CG * P) <= ACCW and N + (NT - NR) + WIN <= ACCW

    x1_dram = nc.dram_tensor("x1_by_node", (N, D), F32).ap()
    rec_dram = nc.dram_tensor("sorted_edges", (E, DE + 2), F32).ap()
    next_dram = nc.dram_tensor("next_place", (N + P, 1), F32).ap()
    r0_dram = nc.dram_tensor("first_rank", (NT, 1), I32).ap()
    tile_dst = nc.dram_tensor("dst_by_tile", (NT, P), I32).ap()
    rk_dram = nc.dram_tensor("first_rank_of_chunk", (RC, 1), I32).ap()
    d_dram = nc.dram_tensor("tile_offset", (NB, BT), I32).ap()

    def alone(eng, s, value):
        eng.wait_ge(s, value)
        eng.sem_inc(passed, 1)

    with ExitStack() as ctx:
        def sb(name, shape, dt=F32):
            return ctx.enter_context(nc.sbuf_tensor(name, shape, dt))

        def psum(name, shape):
            return ctx.enter_context(nc.psum_tensor(name, shape, F32))

        def sem(name):
            return ctx.enter_context(nc.semaphore(name))

        acc = sb("acc", [P, ACCW])
        G = sb("G", [P, 2 * BT * D])
        idx = sb("idx", [P, NT + BT], I32)
        idxg = sb("idxg", [P, 2, BT], I32)
        rel = sb("rel", [P, NT])
        dst_i = sb("dst_i", [BT, NB, P], I32)
        st = sb("st", [BT, NB, P], BF16)
        r0row = sb("r0row", [1, NB * BB], I32)
        drow = sb("drow", [1, NT], I32)
        prev_i = sb("prev_i", [BT, NB], I32)
        fall_q = sb("fall_q", [BT, 2])
        flag = sb("flag", [1, 1], I32)
        resets = sb("resets", [BT, NB, 3])
        pack3 = sb("pack3", [BT, 3])
        row3 = sb("row3", [1, 3, P])
        rowR = sb("rowR", [1, BT])
        inner = sb("inner", [BT, NB])
        cnt = sb("cnt", [BT, NB])
        st0 = sb("st0", [BT, NB])
        ident = sb("ident", [P, P])
        identb = sb("identb", [P, P], BF16)
        iota = sb("iota", [P, P])
        pidx = sb("pidx", [P, 1])
        dump = sb("dump", [P, 1])
        onesr = sb("onesr", [P, P])
        low = sb("low", [NB, NB])
        base0 = sb("base0", [NB, 1])
        r0i = sb("r0i", [NB, BT], I32)
        di = sb("di", [NB, BT], I32)
        srcf = sb("srcf", [BT, P])
        relrow = sb("relrow", [BT, P])
        fcw = sb("fcw", [D, D])
        acol = sb("acol", [D, 2])
        vsb = sb("vsb", [P, D])
        vdb = sb("vdb", [P, D])
        ED = sb("ED", [NHI, P])
        EDr = sb("EDr", [NHI, P])
        EDp = sb("EDp", [NHI, 3, P], BF16)
        R0 = sb("R0", [C0, C0])
        R1 = sb("R1", [C1, D + 1])
        SW = sb("SW", [D + 1, D])
        loi = sb("loi", [BT, P], I32)
        lof = sb("lof", [BT, P])
        hii = sb("hii", [BT, P], I32)
        hib = sb("hib", [BT, P], BF16)
        stdr = sb("stdr", [BT, P])
        negst = sb("negst", [BT, P + 1])
        loT = sb("loT", [P, BT])
        stT = sb("stT", [P, BT])
        WD = sb("WD", [P, BT, 2])
        HY = sb("HY", [NHI, 2, WIN], BF16)
        L0 = sb("L0", [P, 2 * QT * C0 + QT * (P + D) + 5 * P + 2 * BT])
        OH = sb("OH", [NHI, 2, WIN], BF16)
        nhi = sb("nhi", [P, 1])
        zrow = sb("zrow", [1, WIN], BF16)
        es = sb("es", [P, BT])
        ed = sb("ed", [P, BT])
        fr = sb("fr", [1, 1])
        Kin = sb("Kin", [BT, 1])
        rowH = sb("rowH", [1, BT + 1])
        rowK = sb("rowK", [1, BT])
        Cin = sb("Cin", [BT, 1])
        rowC = sb("rowC", [1, BT + 1])
        Fs = sb("Fs", [C0, 1])
        fscale = sb("fscale", [C0, 1])
        U = sb("U", [P, NS, QT, P])
        nz = sb("nz", [P, 2, CG])
        den = sb("den", [P, 2, CG])
        rcp = sb("rcp", [P, 2, CG])
        idW = sb("idW", [P, RC])
        chunk0 = sb("chunk0", [P, RC])
        mean = sb("mean", [P, 2, CG])
        var = sb("var", [P, 2, CG])
        sd = sb("sd", [P, 2, CG])
        rstd = sb("rstd", [P, 2, CG])
        chunk_f = sb("chunk_f", [RC, 4])
        last_t = sb("last_t", [RC, 1], I32)
        last_r0 = sb("last_r0", [RC, 1], I32)
        rk_i = sb("rk_i", [RC, 1], I32)
        early3 = sb("early3", [1, len(EARLY)])
        early = sb("early", [1, 1], I32)
        rkrow = sb("rkrow", [1, RC], I32)
        eps = sb("eps", [P, 1])

        HB = psum("HB", [P, 1024])
        EDP = psum("EDP", [P, 1024])
        MP = psum("MP", [P, 1536])
        PF = psum("PF", [P, 512])

        cT, sT, cum, tmp0 = [acc[0:NB, 11776 + k * BT:11776 + (k + 1) * BT] for k in range(4)]
        taken = [0]

        def part(parts, *shape):
            size = 1
            for k in shape:
                size *= k
            v = L0[0:parts, taken[0]:taken[0] + size]
            taken[0] += size
            if len(shape) == 2:
                v = v.rearrange("p (a b) -> p a b", a=shape[0])
            if len(shape) == 3:
                v = v.rearrange("p (a b c) -> p a b c", a=shape[0], b=shape[1])
            return v

        SR = part(P, 2, QT, C0)
        selj = part(P, QT, P)
        esx = part(P, QT, D)
        F1, F2, M, wr, Bh = [part(BT, P) for _ in range(5)]
        S0, S = part(P, BT), part(P, BT)
        ring = G[:, BT * D:BT * D + RG * QT * C1].rearrange("p (t c) -> p t c", c=C1)
        xs = L0[:, 0:D]
        xT = L0[0:D + 1, D:D + P]
        Gt = G[:, :].rearrange("p (t d) -> p t d", d=D)
        src_i = acc[0:BT, 8192:8192 + NB * P].bitcast(I32).rearrange("q (b e) -> q b e", e=P)
        xhi = acc[0:NHI, 0:P * D]
        xv = G[:, 0:RC * D].rearrange("p (c d) -> p c d", d=D)
        accS = [dst_i[0:C1, :, :].rearrange("q b e -> q (b e)")[:, k * CG * P:(k + 1) * CG * P].bitcast(F32) for k in range(2)]
        H = D + P
        oh_n = [L0[:, H + k * CG * P:H + (k + 1) * CG * P].rearrange("p (c r) -> p c r", r=P) for k in range(2)]
        H = BT * D + RG * QT * C1
        rows_n = [G[:, H + k * CG * D:H + (k + 1) * CG * D].rearrange("p (c d) -> p c d", d=D) for k in range(2)]
        H += 2 * CG * D
        sqv = [G[:, H + k * CG * D:H + (k + 1) * CG * D].rearrange("p (c d) -> p c d", d=D) for k in range(2)]
        earlier = acc[0:BT, 0:RC * NB].rearrange("q (c b) -> q c b", b=NB)
        n_earlier = acc[0:BT, RC * NB:RC * NB + RC]
        row_i, row_f = EDr[:, :].bitcast(I32), ED
        starts_n, before_n = F1[0:RC, 0:P - 1], F2[0:RC, 0:P - 1]
        MPb = [MP[:, 512 * k:512 * (k + 1)] for k in range(3)]
        B = [HB[:, 0:512], HB[:, 512:1024], EDP[:, 0:512], EDP[:, 512:1024], PF[:, :]]
        HBb = [B[0], B[1]]
        EDb = [B[k].rearrange("p (j r) -> p j r", r=P) for k in (2, 3)]
        LO_T, ID_T, ROWS = B[0][:, 0:BT], B[1][:, 0:BT], B[2][0:1, 0:3 * P].rearrange("o (k q) -> o k q", k=3)
        S_T, TAILR, HEADR, W_T = B[2][0:BT, 0:P], B[0][0:1, 0:BT], B[1][0:1, 0:BT], B[3][:, 0:BT]
        CINC, CINK, FB = B[0][0:BT, 0:1], B[1][0:BT, 0:1], B[4][0:C0, 0:1]
        HP = [HB[:, 0:CG * C0].rearrange("p (j c) -> p j c", c=C0),
              HB[:, 512:512 + CG * C0].rearrange("p (j c) -> p j c", c=C0)]
        HQ = [HB[:, 0:CG * (D + 1)].rearrange("p (j c) -> p j c", c=D + 1),
              HB[:, 512:512 + CG * (D + 1)].rearrange("p (j c) -> p j c", c=D + 1)]
        HN = [EDP[:, 512 * k:512 * k + CG * D].rearrange("p (j c) -> p j c", c=D) for k in range(2)]

        eye_d, same, below, sortj = [G[:, k * P:(k + 1) * P] for k in range(4)]
        rec = G[:, 512:512 + DE + 2]
        (dst_f, total, rank, now, new, last_f, gap, count0) = [G[:, 560 + k:561 + k] for k in range(8)]
        dst_c, place_i, keep_i = [G[:, 570 + k:571 + k].bitcast(I32) for k in range(3)]
        counts, upto, zeros_n = [G[0:NP, 600 + k * NJ:600 + (k + 1) * NJ] for k in range(3)]
        tri = G[0:NP, 1024:1024 + NP]

        falls, falls_ps, flag_ready = sem("falls"), sem("falls_ps"), sem("flag_ready")
        so_dst, so_dve, so_pe, so_got, so_kept = [[sem(f"{name}{k}") for k in range(2)]
                                                  for name in ("so_dst", "so_dve", "so_pe", "so_got", "so_kept")]
        so_rec, so_placed = [sem(f"so_rec{k}") for k in range(3)], sem("so_placed")
        so_set, so_zero, so_cnt, so_cntd, so_cntp, reload = (
            sem("so_set"), sem("so_zero"), sem("so_cnt"), sem("so_cntd"), sem("so_cntp"), sem("reload"))
        passed, rescaled = sem("passed"), sem("rescaled")
        idx_copied, idx1_ready = sem("idx_copied"), sem("idx1_ready")
        ld_dst, ld_src, first_src, first_p = sem("ld_dst"), sem("ld_src"), sem("first_src"), sem("first_p")
        ld_prev, ld_w, ld_xhi = sem("ld_prev"), sem("ld_w"), sem("ld_xhi")
        prev_set, xhi_set, consts = sem("prev_set"), sem("xhi_set"), sem("consts")
        pro, pro_t = sem("pro"), sem("pro_t")
        set_d, set_p, acc_zero, acc_zero1 = sem("set_d"), sem("set_p"), sem("acc_zero"), sem("acc_zero1")
        r0_done, r0_st, r0_ld = sem("r0_done"), sem("r0_st"), sem("r0_ld")
        gathered = [sem(f"gathered{g}") for g in range(NG)]
        prep, prep_t = sem("prep"), sem("prep_t")
        pads, hb_used = sem("pads"), sem("hb_used")
        hb_ready, onehot_hi, ed_ready, ed_free, es_prod, es_ready = (
            sem("hb_ready"), sem("onehot_hi"), sem("ed_ready"), sem("ed_free"), sem("es_prod"), sem("es_ready"))
        sm, sm_t, exp_ready = sem("sm"), sem("sm_t"), sem("exp_ready")
        rows_scaled, onehots, agg, mp_free = sem("rows_scaled"), sem("onehots"), sem("agg"), sem("mp_free")
        tables_st, last_set, row_got, chunk_r, rk_set, rk_st, rk_ld, early_set = (
            sem("tables_st"), sem("last_set"), sem("row_got"), sem("chunk_r"), sem("rk_set"), sem("rk_st"), sem("rk_ld"), sem("early_set"))
        ld_x, x_pad = sem("ld_x"), sem("x_pad")
        staged, rk_p, rows_s, rows_r, node_p, centred, squared, var_r, sd_r, norm_s, node_st = [
            [sem(f"{name}{k}") for k in range(2)]
            for name in ("staged", "rk_p", "rows_s", "rows_r", "node_p", "centred", "squared", "var_r", "sd_r",
                         "norm_s", "node_st")]
        ring_ones, sw_ready = sem("ring_ones"), sem("sw_ready")
        g1 = [sem(f"g1_{s}") for s in range(RG)]
        at1 = [sem(f"at1_{h}") for h in range(2)]
        u1, agg1, mp1_free = sem("u1"), sem("agg1"), sem("mp1_free")
        xs_r, xst_r, xT_r, y_p, y_r = sem("xs_r"), sem("xst_r"), sem("xT_r"), sem("y_p"), sem("y_r")

        block = ctx.enter_context(nc.Block())

        def by_tile(e):
            n = (NB - 1) * BT * P
            return e[0:n].rearrange("(b q e) -> q b e", q=BT, e=P), e[n:E].rearrange("(q e) -> q e", e=P)

        at_given = edge_attr.rearrange("(t e) f -> e t f", e=P)
        at_sorted = rec_dram[:, 0:DE].rearrange("(t e) f -> e t f", e=P)

        def if_unsorted(eng):
            eng.wait_ge(flag_ready, 1)
            return eng.If(eng.value_load(flag[0:1, 0:1], min_val=0, max_val=1) > 0)

        full_rows = (RC - 1) * P

        def move_nodes(eng, table, to_table, done, c, n):
            t = table[0:full_rows, :].rearrange("(c p) d -> p c d", p=P)[:, bass.ds(c, n), :]
            v = xv[:, bass.ds(c, n), :]
            eng.dma_start(*((t, v) if to_table else (v, t))).then_inc(done, 16)

        def move_last(eng, table, to_table, done):
            move_nodes(eng, table, to_table, done, (NCG - 1) * CG, CG - 1)
            t, v = table[full_rows:N, :], xv[0:TAIL, RC - 1, :]
            eng.dma_start(*((t, v) if to_table else (v, t))).then_inc(done, 16)

        MOVED = (NCG + 1) * 16

        def in_turn(eng, stages, L, start=0, stop=NCG):
            far = max(behind for _, behind in stages)
            steady = start + far + far % 2

            def one(g, k, peeled):
                for stage, behind in stages:
                    if not peeled or start <= g - behind < stop:
                        stage(L, g - behind, (k - behind) % 2)

            if steady >= stop:
                steady = stop
            for g in range(start, steady):
                one(g, g % 2, True)
            if steady < stop:
                with eng.Fori(steady // 2, stop // 2) as i:
                    for k in range(2):
                        one(i * 2 + k, k, False)
            for g in range(stop, stop + far):
                one(g, g % 2, True)

        def if_early(eng):
            eng.wait_ge(early_set, 3)
            return eng.If(eng.value_load(early[0:1, 0:1], min_val=0, max_val=1) > 0)

        def last_rounds(eng, rounds, to_nodes, rest):
            with if_early(eng):
                for n, (first, groups) in enumerate(EARLY):
                    to_nodes(first, *groups)
                    rounds(first, EARLY[n + 1][0] if n + 1 < len(EARLY) else R1N, True)
                rest()
                to_nodes(None, LAST_EARLY, NCG)
            with eng.Else():
                rounds(EARLY[0][0], R1N, False)
                rest()
                to_nodes(None, 0, NCG)

        @block.sync
        def _(sp):
            with nc.allow_non_contiguous_dma(reason="one word per tile, and columns of weights"):
                sp.wait_ge(pads, 2)
                for t, e, ld in ((dst_i[:, :, :], dst, ld_dst), (src_i, src, ld_src)):
                    full, rest = by_tile(e)
                    sp.dma_start(t[:, 0:NB - 1, :], full).then_inc(ld, 16)
                    sp.dma_start(t[0:LASTQ, NB - 1, :], rest).then_inc(ld, 16)
                full, rest = by_tile(dst)
                sp.wait_ge(prev_set, 1)
                sp.dma_start(prev_i[1:BT, 0:NB - 1].unsqueeze(2), full[0:BT - 1, :, P - 1:P]).then_inc(ld_prev, 16)
                sp.dma_start(prev_i[0:1, 1:NB].unsqueeze(2), full[BT - 1:BT, :, P - 1:P]).then_inc(ld_prev, 16)
                sp.dma_start(prev_i[1:LASTQ, NB - 1:NB], rest[0:LASTQ - 1, P - 1:P]).then_inc(ld_prev, 16)
                sp.dma_start(fcw[:, :], fc_w).then_inc(ld_w, 16)
                sp.dma_start(acol[:, 0:1], attn_w[0, 0:D].unsqueeze(1)).then_inc(ld_w, 16)
                sp.dma_start(acol[:, 1:2], attn_w[0, D:2 * D].unsqueeze(1)).then_inc(ld_w, 16)
            with if_unsorted(sp):
                sp.wait_ge(so_set, 1)
                sp.dma_start(next_dram[0:N, 0].rearrange("(p j) -> p j", p=NP), zeros_n).then_inc(so_zero, 16)
                sp.dma_start(next_dram[N:N + P, :], count0).then_inc(so_zero, 16)
                sp.wait_ge(so_zero, 32)

                def load_edges(t, placing):
                    with nc.allow_non_contiguous_dma(reason="an edge on each partition"):
                        sp.dma_start(dst_c, dst[bass.ds(t * P, P)].unsqueeze(1)).then_inc(so_dst[placing], 16)
                        if placing:
                            sp.dma_start(rec[:, DE:DE + 1].bitcast(I32), src[bass.ds(t * P, P)].unsqueeze(1)).then_inc(so_rec[0], 16)
                            sp.dma_start(rec[:, DE + 1:DE + 2].bitcast(I32), dst[bass.ds(t * P, P)].unsqueeze(1)).then_inc(so_rec[1], 16)
                            sp.dma_start(rec[:, 0:DE], edge_attr[bass.ds(t * P, P), :]).then_inc(so_rec[2], 16)

                with sp.Fori(0, NR) as t:
                    load_edges(t, False)
                    alone(sp, so_kept[0], (t + 1) * 16)
                sp.dma_start(counts, next_dram[0:N, 0].rearrange("(p j) -> p j", p=NP)).then_inc(so_cnt, 16)
                sp.wait_ge(so_cntd, 3)
                sp.dma_start(next_dram[0:N, 0].rearrange("(p j) -> p j", p=NP), counts).then_inc(so_cnt, 16)
                sp.wait_ge(so_cnt, 32)
                with sp.Fori(0, NR) as t:
                    load_edges(t, True)
                    alone(sp, so_kept[1], (t + 1) * 16)
                    alone(sp, so_placed, (t + 1) * 16)
                with nc.allow_non_contiguous_dma(reason="one word of each record"):
                    by_edge = rec_dram.bitcast(I32)
                    for t, e in ((src_i, by_edge[:, DE]), (dst_i[:, :, :], by_edge[:, DE + 1])):
                        full, rest = by_tile(e)
                        for c in range(NB - 1):
                            sp.dma_start(t[:, c, :].unsqueeze(2), full[:, c, :].unsqueeze(2)).then_inc(reload, 16)
                        sp.dma_start(t[0:LASTQ, NB - 1, :].unsqueeze(2), rest.unsqueeze(2)).then_inc(reload, 16)
                    full, rest = by_tile(by_edge[:, DE + 1])
                    sp.dma_start(prev_i[1:BT, 0:NB - 1].unsqueeze(2), full[0:BT - 1, :, P - 1:P]).then_inc(reload, 16)
                    sp.dma_start(prev_i[0:1, 1:NB].unsqueeze(2), full[BT - 1:BT, :, P - 1:P]).then_inc(reload, 16)
                    sp.dma_start(prev_i[1:LASTQ, NB - 1:NB], rest[0:LASTQ - 1, P - 1:P]).then_inc(reload, 16)
                sp.wait_ge(reload, (2 * NB + 3) * 16)
            sp.wait_ge(xhi_set, 1)
            sp.dma_start(xhi[0:NHI - 1, :], x[0:(NHI - 1) * P, :].rearrange("(h l) d -> h (l d)", l=P)).then_inc(ld_xhi, 16)
            sp.dma_start(xhi[NHI - 1:NHI, 0:TAIL * D],
                         x[(NHI - 1) * P:N, :].rearrange("(h l) d -> h (l d)", h=1)).then_inc(ld_xhi, 16)
            sp.dma_start(R1[0:D + DE, 0:D], msg_w).then_inc(ld_w, 16)
            sp.dma_start(R1[D + DE:C1, 0:D], msg_b.unsqueeze(0)).then_inc(ld_w, 16)
            sp.dma_start(SW[0:D, :], self_w).then_inc(ld_w, 16)
            sp.dma_start(SW[D:D + 1, :], self_b.unsqueeze(0)).then_inc(ld_w, 16)
            sp.wait_ge(r0_done, 1)
            sp.dma_start(r0_dram.rearrange("(b t) o -> b (t o)", b=NB), r0i[:, :]).then_inc(r0_st, 16)
            sp.dma_start(d_dram, di[:, :]).then_inc(r0_st, 16)
            sp.wait_ge(r0_st, 32)
            with nc.allow_non_contiguous_dma(reason="first tile of each batch"):
                sp.dma_start(r0row[0:1, :].unsqueeze(2),
                             r0_dram.rearrange("(n j) o -> o n j", j=QT)[:, :, 0:1]).then_inc(r0_ld, 16)
            sp.dma_start(drow[0:1, :], d_dram.rearrange("b t -> (b t)").unsqueeze(0)).then_inc(r0_ld, 16)
            sp.dma_start(tile_dst.rearrange("(b q) e -> q b e", q=BT), dst_i[:, :, :]).then_inc(tables_st, 16)
            sp.wait_ge(rk_set, 1)
            sp.dma_start(rk_dram, rk_i[:, :]).then_inc(rk_st, 16)
            sp.wait_ge(rk_st, 16)
            sp.dma_start(rkrow[0:1, :], rk_dram.rearrange("c o -> o c")).then_inc(rk_ld, 16)
            sp.wait_ge(x_pad, 1)
            with sp.Fori(0, NCG - 1) as c7:
                move_nodes(sp, x, False, ld_x, c7 * CG, CG)
            move_last(sp, x, False, ld_x)
            with sp.Fori(0, NCG - 1) as c7:
                alone(sp, norm_s[0], (c7 + 1) * 2)
                move_nodes(sp, x1_dram, True, node_st[0], c7 * CG, CG)
            sp.wait_ge(norm_s[0], NCG * 2)
            move_last(sp, x1_dram, True, node_st[0])
            def load_attrs(attr):
                def load_attr(i, h, tiles):
                    sp.wait_ge(agg1, i * RG + (h + 1) * HG)
                    sp.dma_start(ring[:, h * HG * QT:h * HG * QT + tiles, D:D + DE],
                                 attr[:, bass.ds((i * RG + h * HG) * QT, tiles), :]).then_inc(at1[h], 16)

                with sp.Fori(0, R1N) as i:
                    for h in range(2):
                        load_attr(i, h, HG * QT)
                load_attr(R1N, 0, QT + 1)

            with if_unsorted(sp):
                load_attrs(at_sorted)
            with sp.Else():
                load_attrs(at_given)
            with sp.Fori(0, NCG - 1) as c7:
                alone(sp, norm_s[1], (c7 + 1) * 2)
                move_nodes(sp, out, True, node_st[1], c7 * CG, CG)
            sp.wait_ge(norm_s[1], NCG * 2)
            move_last(sp, out, True, node_st[1])
            sp.wait_ge(node_st[1], MOVED)

        @block.gpsimd
        def _(g):
            c = Steps(g, consts)
            g.memset(dst_i[EMPTY:BT, NB - 1, :], -1).then_inc(pads, 1)
            g.wait_ge(pads, 1)
            g.memset(src_i[EMPTY:BT, NB - 1, :], 0).then_inc(pads, 1)
            g.wait_ge(pads, 2)
            g.memset(prev_i[:, :], -2).then_inc(prev_set, 1)
            g.wait_ge(prev_set, 1)
            g.memset(xhi[(NHI - 1) // 32 * 32:NHI, TAIL * D:P * D], 0.0).then_inc(xhi_set, 1)
            g.wait_ge(xhi_set, 1)
            for tile, value in ((onesr, 1.0), (eps, EPS), (rowC, NEG), (rowH, NEG), (relrow, 0.0), (negst, 0.0), (fscale, 1.0),
                                (ident, 0.0)):
                c.did(g.memset(tile[:, :], value))
                c.wait()
            for tile, pattern, first, by_partition in ((iota, [[1, P]], 0, 0), (pidx, [[0, 1]], 0, 1), (dump, [[0, 1]], N, 1), (chunk0, [[P, RC]], 0, 0)):
                c.did(g.iota(tile[:, :], pattern=pattern, base=first, channel_multiplier=by_partition,
                             allow_small_or_imprecise_dtypes=True))
                c.wait()
            c.did(g.affine_select(out=ident[:, :], in_=ident[:, :], compare_op=ALU.not_equal, fill=1.0,
                                  base=0, pattern=[[-1, P]], channel_multiplier=1))
            c.wait()
            c.did(g.affine_select(out=fscale[:, :], in_=fscale[:, :], compare_op=ALU.not_equal, fill=0.0,
                                  base=-(D + 1), pattern=[[0, 1]], channel_multiplier=1))
            assert c.n == NCONST

            with if_unsorted(g):
                for placing in (False, True):
                    with g.Fori(0, NR) as t:
                        alone(g, so_dve[placing], t * 11 + 8)
                        g.indirect_dma_start(now, None, next_dram[:, :],
                                             bass.IndirectOffsetOnAxis(ap=dst_c, axis=0)).then_inc(so_got[placing], 16)
                        alone(g, so_dve[placing], t * 11 + 11)
                        if placing:
                            for q in so_rec:
                                alone(g, q, (t + 1) * 16)
                            g.indirect_dma_start(rec_dram[:, :], bass.IndirectOffsetOnAxis(ap=place_i, axis=0),
                                                 rec, None).then_inc(so_placed, 16)
                        g.indirect_dma_start(next_dram[:, :], bass.IndirectOffsetOnAxis(ap=keep_i, axis=0),
                                             new, None).then_inc(so_kept[placing], 16)
                        alone(g, so_kept[placing], (t + 1) * 16)
                        if placing:
                            alone(g, so_placed, (t + 1) * 16)

            def gather_block(b, half, tiles=BT):
                alone(g, idx_copied, b + 1)
                for k in range(NG):
                    alone(g, rows_scaled, b * BB + (k + 1) * GB)
                    alone(g, es_ready, b * BB + (k + 1) * GB + 1)
                    for j in range(min(GT, tiles - k * GT)):
                        g.indirect_dma_start(Gt[:, half * BT + k * GT + j, :], None, x[:, :],
                                             bass.IndirectOffsetOnAxis(ap=idxg[:, half, k * GT + j:k * GT + j + 1], axis=0)
                                             ).then_inc(gathered[k], 16)

            with g.Fori(0, NB // 2 - 1) as b2:
                for half in range(2):
                    gather_block(b2 * 2 + half, half)
            gather_block(NB - 2, 0)
            gather_block(NB - 1, 1, LASTQ)

            g.wait_ge(last_set, 1)
            g.wait_ge(tables_st, 16)
            g.indirect_dma_start(row_i, None, tile_dst[:, :],
                                 bass.IndirectOffsetOnAxis(ap=last_t[:, 0:1], axis=0)).then_inc(row_got, 16)
            g.indirect_dma_start(last_r0[:, :], None, r0_dram[:, :],
                                 bass.IndirectOffsetOnAxis(ap=last_t[:, 0:1], axis=0)).then_inc(row_got, 16)
            g.wait_ge(rows_scaled, (NB - 1) * BB + 2 * BB)
            g.memset(xv[64:P, RC - 1, :], 0.0).then_inc(x_pad, 1)

            g.wait_ge(node_st[0], MOVED)
            g.wait_ge(ring_ones, 1)

            def gather1(i, h, tiles):
                alone(g, idx1_ready, i * 2 + h + 1)
                for j in range(tiles):
                    g.indirect_dma_start(ring[:, h * HG * QT + j, 0:D], None, x1_dram[:, :],
                                         bass.IndirectOffsetOnAxis(ap=idxg[:, h, j:j + 1], axis=0)
                                         ).then_inc(g1[h * HG + j // QT], 16)

            with g.Fori(0, R1N) as i:
                for h in range(2):
                    gather1(i, h, HG * QT)
            gather1(R1N, 0, QT + 1)

        @block.vector
        def _(v):
            for free, buffers in ((es_ready, 1 + BB), (ed_free, 2), (rows_scaled, 2 * BB), (agg, 2), (agg1, RG),
                                  (mp_free, 2), (mp1_free, NS), (hb_used, 2), (onehot_hi, 2), (ed_ready, 2),
                                  *[(s, 2) for s in rk_p + rows_r + node_p], *[(s, 6) for s in centred]):
                v.sem_inc(free, buffers)

            d = Steps(v, set_d)
            v.wait_ge(consts, NCONST)
            d.did(v.tensor_copy(identb[:, :], ident[:, :]))
            d.did(v.tensor_tensor(low[:, :], iota[0:NB, 0:NB], pidx[0:NB, 0:1].to_broadcast([NB, NB]), ALU.is_gt))
            v.memset(row3[:, :, :], 0.0)
            v.memset(zrow[:, :], 0.0)
            v.tensor_scalar(nhi[:, :], pidx[:, :], -1.0, None, ALU.mult)
            v.wait_ge(ld_dst, 32)
            v.wait_ge(ld_prev, 48)
            v.scalar_tensor_tensor(out=st[:, :, 1:P], in0=dst_i[:, :, 1:P], scalar=1.0, in1=dst_i[:, :, 0:P - 1],
                                   op0=ALU.mult, op1=ALU.is_lt, accum_out=fall_q[:, 0:1])
            v.scalar_tensor_tensor(out=st[:, :, 0:1], in0=dst_i[:, :, 0:1], scalar=1.0, in1=prev_i[:, :].unsqueeze(2),
                                   op0=ALU.mult, op1=ALU.is_lt, accum_out=fall_q[:, 1:2]).then_inc(falls, 1)
            v.wait_ge(falls_ps, 1)
            v.tensor_scalar(flag[:, :], B[0][0:1, 0:1], 0.0, None, ALU.is_gt).then_inc(flag_ready, 1)
            with if_unsorted(v):
                v.memset(zeros_n, 0.0)
                v.memset(count0, 0.0)
                v.tensor_tensor(tri, iota[0:NP, 0:NP], pidx[0:NP, 0:1].to_broadcast([NP, NP]), ALU.is_gt)
                v.tensor_tensor(below, iota[:, :], pidx[:, 0:1].to_broadcast([P, P]), ALU.is_lt).then_inc(so_set, 1)
                v.wait_ge(so_set, 1)
                for placing in (False, True):
                    with v.Fori(0, NR) as t:
                        p = Steps(v, so_dve[placing], t * 11)
                        v.wait_ge(so_dst[placing], (t + 1) * 16)
                        p.did(v.tensor_copy(dst_f, dst_c))
                        p.wait()
                        p.did(v.tensor_scalar(eye_d, ident[:, :], dst_f, None, ALU.mult))
                        v.wait_ge(so_pe[placing], t + 1)
                        p.did(v.tensor_scalar(same, B[0][:, 0:P], dst_f, None, ALU.is_equal))
                        p.wait()
                        p.did(v.tensor_reduce(total, same, AX_X, ALU.add))
                        p.did(v.tensor_tensor(sortj, same, below, ALU.mult))
                        p.wait()
                        p.did(v.tensor_reduce(rank, sortj, AX_X, ALU.add))
                        p.wait()
                        p.did(v.tensor_tensor(gap, total, rank, ALU.subtract))
                        p.wait()
                        p.did(v.tensor_scalar(last_f, gap, 1.0, None, ALU.is_equal))
                        p.wait()
                        v.wait_ge(so_got[placing], (t + 1) * 16)
                        p.did(v.tensor_tensor(gap, dst_f, dump[:, :], ALU.subtract))
                        v.tensor_tensor(place_i, now, rank, ALU.add)
                        v.tensor_tensor(new, now, total, ALU.add)
                        p.wait()
                        p.did(v.tensor_tensor(gap, gap, last_f, ALU.mult))
                        p.wait()
                        p.did(v.tensor_tensor(keep_i, gap, dump[:, :], ALU.add))
                        v.wait_ge(so_kept[placing], (t + 1) * 16)
                        if placing:
                            alone(v, so_placed, (t + 1) * 16)
                    if not placing:
                        v.wait_ge(so_cnt, 16)
                        v.tensor_tensor_scan(upto, onesr[0:NP, 0:NJ], counts, 0.0, ALU.mult, ALU.add).then_inc(so_cntd, 1)
                        v.wait_ge(so_cntd, 1)
                        v.tensor_tensor(counts, upto, counts, ALU.subtract).then_inc(so_cntd, 1)
                        v.wait_ge(so_cntp, 1)
                        v.tensor_copy(count0[0:NP, :], B[1][0:NP, 0:1]).then_inc(so_cntp, 1)
                        v.wait_ge(so_cntp, 2)
                        v.wait_ge(so_cntd, 2)
                        v.tensor_scalar(counts, counts, count0[0:NP, :], None, ALU.add).then_inc(so_cntd, 1)
                v.wait_ge(reload, (2 * NB + 3) * 16)
            v.wait_ge(ld_src, 32)
            v.tensor_copy(srcf[:, :], src_i[:, 0, :])
            v.tensor_copy(lof[:, :], src_i[:, 1, :]).then_inc(first_src, 1)
            for b in range(2):
                v.wait_ge(first_p, b + 1)
                v.tensor_copy(idxg[:, b, :], B[b + 1][:, 0:BT]).then_inc(idx_copied, 1)
            v.tensor_tensor(st[:, :, 1:P], dst_i[:, :, 1:P], dst_i[:, :, 0:P - 1], ALU.not_equal)
            v.tensor_tensor(st[:, :, 0:1], dst_i[:, :, 0:1], prev_i[:, :].unsqueeze(2), ALU.not_equal)
            d.did(v.tensor_tensor(st0[:, :].unsqueeze(2), dst_i[:, :, 0:1], prev_i[:, :].unsqueeze(2), ALU.not_equal))
            d.wait()
            v.memset(idx[:, NT:NT + BT], 0)

            def ranks_of_block(b):
                p = Steps(v, pro, b * 5)
                q = Steps(v, pro_t, b * 2)
                p.did(v.tensor_copy(srcf[:, :], src_i[:, b, :]))
                p.did(v.tensor_tensor_scan(relrow[:, 1:P], onesr[0:BT, 0:P - 1], st[:, b, 1:P], 0.0, ALU.mult, ALU.add))
                p.wait()
                p.did(v.tensor_tensor(cnt[:, bass.ds(b, 1)], relrow[:, P - 1:P], st0[:, bass.ds(b, 1)], ALU.add))
                q.wait(1)
                p.did(v.tensor_copy(idx[:, bass.ds(b * BT, BT)], B[0][:, 0:BT]))
                q.wait(2)
                p.did(v.tensor_copy(rel[:, bass.ds(b * BT, BT)], B[1][:, 0:BT]))
                p.wait()

            with v.Fori(0, NB) as b:
                ranks_of_block(b)

            v.wait_ge(pro, NB * 5)
            v.memset(rel[:, NR:NT], -1.0)
            v.tensor_tensor(inner[:, :], cnt[:, :], st0[:, :], ALU.subtract)
            v.tensor_scalar(resets[:, :, 0], cnt[:, :], 0.0, NEG, ALU.is_gt, ALU.mult)
            d.did(v.tensor_scalar(resets[:, :, 2], st0[:, :], NEG, None, ALU.mult))
            d.wait()
            v.tensor_scalar(resets[:, :, 1], inner[:, :], 0.0, NEG, ALU.is_gt, ALU.mult)
            v.wait_ge(set_p, 2)
            v.tensor_copy(cT[:, :], B[0][0:NB, 0:BT])
            d.did(v.tensor_copy(sT[:, :], B[0][0:NB, 128:128 + BT]))
            d.wait()
            d.did(v.tensor_tensor_scan(cum[:, :], onesr[0:NB, 0:BT], cT[:, :], 0.0, ALU.mult, ALU.add))
            d.wait()
            d.did(v.tensor_tensor(tmp0[:, :], cum[:, :], cT[:, :], ALU.subtract))
            v.wait_ge(set_p, 3)
            d.did(v.tensor_copy(base0[:, :], B[1][0:NB, 0:1]))
            d.wait()
            d.did(v.tensor_tensor(cum[:, :], tmp0[:, :], sT[:, :], ALU.add))
            d.wait()
            v.tensor_scalar(r0i[:, :], cum[:, :], base0[:, 0:1], -1.0, ALU.add, ALU.add)
            cum3 = cum[:, :].rearrange("b (n j) -> b n j", j=QT)
            v.tensor_tensor(di[:, :].rearrange("b (n j) -> b n j", j=QT), cum3,
                            cum3[:, :, 0:1].to_broadcast([NB, BB, QT]), ALU.subtract).then_inc(r0_done, 1)

            v.wait_ge(set_p, 6)
            v.tensor_copy(vsb[:, :], B[2][:, 0:D])
            v.tensor_copy(R0[:, :], ident[0:C0, 0:C0])
            v.tensor_copy(R1[:, D:D + 1], ident[0:C1, C1 - 1:C1])
            d.did(v.tensor_copy(vdb[:, :], B[2][:, 128:128 + D]))
            d.wait()
            v.wait_ge(set_p, 6)
            v.tensor_copy(R0[0:D, 0:D], B[2][0:D, 256:256 + D])
            v.wait_ge(ld_xhi, 32)
            xh3 = xhi.rearrange("h (l d) -> h l d", d=D)
            d.did(v.tensor_tensor(xh3, xh3, vdb[0:NHI, :].unsqueeze(1).to_broadcast([NHI, P, D]), ALU.mult))
            d.wait()
            d.did(v.tensor_reduce(ED[:, :], xh3, AX_X, ALU.add))
            d.wait()
            d.did(v.tensor_copy(EDp[:, 0, :], ED[:, :]))
            d.wait()
            d.did(v.tensor_tensor(EDr[:, :], ED[:, :], EDp[:, 0, :], ALU.subtract))
            d.wait()
            d.did(v.tensor_copy(EDp[:, 1, :], EDr[:, :]))
            d.wait()
            d.did(v.tensor_tensor(ED[:, :], EDr[:, :], EDp[:, 1, :], ALU.subtract))
            d.wait()
            d.did(v.tensor_copy(EDp[:, 2, :], ED[:, :]))
            d.did(v.tensor_tensor(earlier, dst_i[:, :, 0:1].rearrange("q b o -> q o b").to_broadcast([BT, RC, NB]),
                                  chunk0[0:BT, :].unsqueeze(2).to_broadcast([BT, RC, NB]), ALU.is_lt))
            d.wait()
            d.did(v.tensor_reduce(n_earlier, earlier, AX_X, ALU.add))
            v.tensor_scalar(chunk_f[:, 0:1], pidx[0:RC, :], float(P), None, ALU.mult)
            v.wait_ge(set_p, 7)
            v.tensor_scalar(chunk_f[:, 1:2], B[3][0:RC, 0:1], float(NT - NR), None, ALU.is_gt)
            v.tensor_scalar(last_t[:, :], B[3][0:RC, 0:1], -float(NT - NR + 1), 0.0, ALU.add, ALU.max).then_inc(last_set, 1)
            v.memset(acc[:, :], 0.0).then_inc(acc_zero, 1)

            def row_forms(b):
                p = Steps(v, prep, b * 11)
                p.did(v.tensor_scalar(loi[:, :], dst_i[:, b, :], P - 1, None, ALU.bitwise_and))
                p.did(v.tensor_scalar(hii[:, :], dst_i[:, b, :], 7, None, ALU.logical_shift_right))
                p.wait()
                p.did(v.tensor_copy(lof[:, :], loi[:, :]))
                p.did(v.tensor_copy(hib[:, :], hii[:, :]))
                p.did(v.tensor_tensor(stdr[:, :], dst_i[:, b, :], st[:, b, :], ALU.mult))
                p.did(v.tensor_scalar(negst[:, 0:P], st[:, b, :], NEG, None, ALU.mult))
                p.did(v.tensor_copy(pack3[:, :], resets[:, b, :]))
                v.wait_ge(prep_t, b * 3 + 1)
                p.did(v.tensor_copy(loT[:, :], LO_T))
                v.wait_ge(prep_t, b * 3 + 2)
                p.did(v.tensor_copy(stT[:, :], ID_T))
                v.wait_ge(prep_t, b * 3 + 3)
                p.did(v.tensor_copy(row3[:, :, 0:BT], ROWS[:, :, 0:BT]))
                p.wait()
                p.did(v.tensor_tensor(rowR[:, :], row3[:, 1, 0:BT], row3[:, 2, 1:BT + 1], ALU.add))
                alone(v, prep, b * 11 + 11)

            def scores(b, i, sl):
                n = b * BB + i
                q0 = i * QT

                def pick(j):
                    return v.scalar_tensor_tensor(out=selj[:, j, :], in0=iota[:, :], scalar=loT[:, bass.ds(q0 + j, 1)],
                                                  in1=EDb[sl][:, j, :], op0=ALU.is_equal, op1=ALU.mult,
                                                  accum_out=ed[:, bass.ds(q0 + j, 1)])

                v.wait_ge(es_ready, n + 1 + BB)
                v.tensor_tensor(esx[:, :, :], Gt[:, bass.ds((b % 2) * BT + q0, QT), :],
                                vsb[:, :].unsqueeze(1).to_broadcast([P, QT, D]), ALU.mult).then_inc(es_prod, 1)
                v.wait_ge(ed_free, n + 2)
                v.wait_ge(ed_ready, n + 3)
                pick(0)
                pick(1)
                v.wait_ge(es_prod, n + 1)
                v.tensor_reduce(es[:, bass.ds(q0, QT)], esx[:, :, :], AX_X, ALU.add).then_inc(es_ready, 1)
                pick(2)
                pick(3).then_inc(ed_free, 1)

            def weigh(b, i, sl):
                n = b * BB + i
                q0 = i * QT
                v.wait_ge(agg, n + 1)
                v.tensor_tensor(SR[:, sl, :, 0:D], Gt[:, bass.ds((b % 2) * BT + q0, QT), :],
                                WD[:, bass.ds(q0, QT), 0:1].to_broadcast([P, QT, D]), ALU.mult).then_inc(rows_scaled, 1)
                v.tensor_copy(SR[:, sl, :, D:C0], WD[:, bass.ds(q0, QT), :])
                v.tensor_tensor(U[:, sl, :, :], iota[:, :].unsqueeze(1).to_broadcast([P, QT, P]),
                                rel[:, bass.ds(b * BT + q0, QT)].unsqueeze(2).to_broadcast([P, QT, P]),
                                ALU.is_equal).then_inc(onehots, 1)

            def maxima(b):
                p = Steps(v, sm, b * 15)
                v.wait_ge(ed_free, (b + 1) * BB + 2)
                p.did(v.tensor_tensor(S0[:, :], es[:, :], ed[:, :], ALU.add))
                p.wait()
                p.did(v.scalar_tensor_tensor(out=S[:, :], in0=S0[:, :], scalar=SLOPE, in1=S0[:, :],
                                             op0=ALU.mult, op1=ALU.max))
                v.wait_ge(sm_t, b * 7 + 1)
                p.did(v.tensor_tensor_scan(F1[:, :], negst[:, 0:P], S_T, NEG, ALU.add, ALU.max))
                p.did(v.tensor_tensor_scan(Bh[:, P - 1::-1], negst[:, P:0:-1], S_T[:, P - 1::-1], NEG, ALU.add, ALU.max))
                v.wait_ge(sm_t, b * 7 + 2)
                p.did(v.tensor_tensor_scan(rowC[0:1, 1:BT + 1], row3[:, 0, 0:BT], TAILR, rowC[0:1, 0:1], ALU.add, ALU.max))
                v.wait_ge(sm_t, b * 7 + 3)
                p.did(v.tensor_tensor_scan(rowH[0:1, BT - 1::-1], rowR[:, BT - 1::-1], HEADR[:, BT - 1::-1], NEG, ALU.add, ALU.max))
                p.wait()
                p.did(v.tensor_tensor(rowK[:, :], rowH[0:1, 1:BT + 1], row3[:, 2, 1:BT + 1], ALU.add))
                v.wait_ge(sm_t, b * 7 + 4)
                p.did(v.tensor_copy(Cin[:, :], CINC))
                v.wait_ge(sm_t, b * 7 + 5)
                p.did(v.tensor_copy(Kin[:, :], CINK))
                p.did(v.tensor_copy(rowC[0:1, 0:1], rowC[0:1, BT:BT + 1]))
                p.wait(9)
                p.did(v.tensor_tensor_scan(F2[:, :], negst[:, 0:P], S_T, Cin[:, 0:1], ALU.add, ALU.max))
                p.wait()
                p.did(v.tensor_tensor_scan(M[:, P - 1::-1], negst[:, P:0:-1], F2[:, P - 1::-1], Kin[:, 0:1], ALU.add, ALU.max))
                p.wait()
                p.did(v.tensor_tensor(wr[:, :], S_T, M[:, :], ALU.subtract))
                p.did(v.tensor_scalar(fr[:, :], Cin[0:1, :], M[0:1, 0:1], 0.0, ALU.subtract, ALU.min))
                v.wait_ge(agg, b * BB + 2)
                p.did(v.tensor_copy(WD[:, :, 1], stT[:, :]))
                alone(v, exp_ready, b * 2 + 1)
                alone(v, sm, b * 15 + 15)

            row_forms(0)
            for k in range(NG):
                v.wait_ge(gathered[k], GT * 16)
                with v.Fori(0, GB // 2) as i:
                    for sl in range(2):
                        scores(0, k * GB + i * 2 + sl, sl)
            maxima(0)
            def sum_and_score(b, empty=0):
                row_forms(b + 1)
                v.tensor_copy(idxg[:, bass.ds(b % 2, 1), :], idx[:, bass.ds((b + 2) * BT, BT)].unsqueeze(1)).then_inc(idx_copied, 1)
                weigh(b, 0, 0)
                for k in range(NG):
                    alone(v, gathered[k], (b + 2) * GT * 16 - (empty * 16 if k == NG - 1 else 0))
                    if k < NG - 1:
                        with v.Fori(0, GB // 2) as i:
                            for sl in range(2):
                                weigh(b, k * GB + i * 2 + sl + 1, 1 - sl)
                                scores(b + 1, k * GB + i * 2 + sl, sl)
                    else:
                        for i in range(k * GB, BB):
                            if i < BB - 1:
                                weigh(b, i + 1, 1 - i % 2)
                            scores(b + 1, i, i % 2)
                maxima(b + 1)

            with v.Fori(0, NB - 2) as b:
                sum_and_score(b)
            sum_and_score(NB - 2, BT - LASTQ)
            c = Steps(v, chunk_r)
            v.wait_ge(row_got, 32)
            c.did(v.tensor_copy(row_f[:, :], row_i))
            c.did(v.tensor_tensor(chunk_f[:, 3:4], last_r0[:, :], onesr[0:RC, 0:1], ALU.add))
            c.wait(1)
            c.did(v.tensor_tensor(starts_n, row_f[:, 1:P], row_f[:, 0:P - 1], ALU.not_equal))
            c.wait()
            c.did(v.scalar_tensor_tensor(out=before_n, in0=row_f[:, 1:P], scalar=chunk_f[:, 0:1], in1=starts_n,
                                         op0=ALU.is_lt, op1=ALU.mult, accum_out=chunk_f[:, 2:3]))
            c.wait()
            c.did(v.tensor_tensor(chunk_f[:, 2:3], chunk_f[:, 2:3], chunk_f[:, 3:4], ALU.add))
            c.wait()
            v.tensor_scalar(rk_i[:, :], chunk_f[:, 2:3], chunk_f[:, 1:2], None, ALU.mult).then_inc(rk_set, 1)
            with v.Fori(0, BB // 2 - 1) as i:
                for sl in range(2):
                    weigh(NB - 1, i * 2 + sl, sl)

            def rows_of_ranks(L, g, k):
                n = 4 if L == 0 else 2
                f = Steps(v, rows_s[L], g * n)
                HPk = HP[k] if L == 0 else HQ[k]
                v.wait_ge(node_p[L], g + 1)
                v.wait_ge(rk_p[L], g + 3)
                if L == 0:
                    f.did(v.tensor_tensor(idW[:, bass.ds(g * CG, CG)], HPk[:, :, D + 1],
                                          chunk0[:, bass.ds(g * CG, CG)], ALU.subtract))
                    f.did(v.tensor_scalar(nz[:, k, :], HPk[:, :, D], 0.0, None, ALU.is_equal))
                    f.wait()
                    f.did(v.tensor_tensor(den[:, k, :], HPk[:, :, D], nz[:, k, :], ALU.add))
                else:
                    f.did(v.tensor_scalar(den[:, k, :], HPk[:, :, D], 1.0, None, ALU.max))
                f.wait()
                f.did(v.reciprocal(rcp[:, k, :], den[:, k, :]))
                f.wait()
                v.tensor_tensor(rows_n[k], HPk[:, :, 0:D],
                                rcp[:, k, :].unsqueeze(2).to_broadcast([P, CG, D]), ALU.mult)
                v.tensor_tensor(oh_n[k], iota[:, :].unsqueeze(1).to_broadcast([P, CG, P]),
                                idW[:, bass.ds(g * CG, CG)].unsqueeze(2).to_broadcast([P, CG, P]),
                                ALU.is_equal).then_inc(rows_r[L], 1)

            def centre(L, g, k):
                f = Steps(v, centred[L], g * 3 + 6)
                z = xv[:, bass.ds(g * CG, CG), :]
                v.wait_ge(node_p[L], g + 3)
                f.did(v.tensor_tensor(z, HN[k], z, ALU.add))
                alone(v, centred[L], g * 3 + 7)
                f.did(v.tensor_reduce(mean[:, k, :], z, AX_X, ALU.add))
                f.wait()
                f.did(v.scalar_tensor_tensor(out=z, in0=mean[:, k, :].unsqueeze(2).to_broadcast([P, CG, D]),
                                             scalar=-1.0 / D, in1=z, op0=ALU.mult, op1=ALU.add))

            def variance(L, g, k):
                v.wait_ge(squared[L], g + 1)
                v.tensor_reduce(var[:, k, :], sqv[k], AX_X, ALU.add).then_inc(var_r[L], 1)

            def normalise(L, g, k):
                f = Steps(v, norm_s[L], g * 2)
                z = xv[:, bass.ds(g * CG, CG), :]
                v.wait_ge(sd_r[L], g + 1)
                f.did(v.reciprocal(rstd[:, k, :], sd[:, k, :]))
                f.wait()
                f.did(v.tensor_tensor(z, z, rstd[:, k, :].unsqueeze(2).to_broadcast([P, CG, D]), ALU.mult))
                f.wait()

            def ranks_to_nodes(L, *groups):
                in_turn(v, ((rows_of_ranks, 0), (centre, 1), (variance, 2), (normalise, 3)), L, *groups)

            v.wait_ge(rk_ld, 16)
            for n, (first, groups) in enumerate(EARLY):
                e = v.tensor_tensor(early3[0:1, n:n + 1], rkrow[0:1, groups[1] * CG:groups[1] * CG + 1],
                                    r0row[0:1, first * RG:first * RG + 1], ALU.is_le)
            e.then_inc(early_set, 1)
            v.wait_ge(early_set, 1)
            v.tensor_reduce(early3[0:1, 0:1], early3[0:1, :], AX_X, ALU.min).then_inc(early_set, 1)
            v.wait_ge(early_set, 2)
            v.tensor_copy(early[:, :], early3[0:1, 0:1]).then_inc(early_set, 1)

            v.wait_ge(ld_x, MOVED)
            ranks_to_nodes(0)
            v.wait_ge(node_st[0], MOVED)
            v.memset(ring[:, :, D + DE:C1], 1.0).then_inc(ring_ones, 1)
            v.memset(xT[D:D + 1, :], 1.0).then_inc(sw_ready, 1)
            v.memset(acc[:, 0:1], 0.0).then_inc(acc_zero1, 1)

            def indices(i, h):
                v.tensor_copy(idxg[:, h, 0:HG * QT], idx[:, bass.ds((i * RG + h * HG) * QT, HG * QT)]).then_inc(idx1_ready, 1)

            def onehots1(n, s, tiles):
                v.wait_ge(agg1, n + 1 + RG - NS)
                v.tensor_tensor(U[:, s % NS, 0:tiles, :], iota[:, :].unsqueeze(1).to_broadcast([P, tiles, P]),
                                rel[:, bass.ds(n * QT, tiles)].unsqueeze(2).to_broadcast([P, tiles, P]),
                                ALU.is_equal).then_inc(u1, 1)

            def round1(i, self_term, filled=False):
                for s in range(RG):
                    onehots1(i * RG + s, s, QT)
                    h, q = s // HG, s % HG
                    if q == NS - 1 and (h or not filled):
                        indices(i + h, 1 - h)
                    if self_term and q == 1:
                        v.wait_ge(xst_r, i * 2 + h + 1)
                        v.tensor_copy(xT[0:D, :], B[0][0:D, 0:P]).then_inc(xT_r, 1)
                    if self_term and q == 3:
                        v.wait_ge(y_p, i * 2 + h + 1)
                        v.tensor_tensor(xv[:, i * 2 + h, :], B[1][:, 0:D], xv[:, i * 2 + h, :], ALU.add).then_inc(y_r, 1)

            indices(0, 0)
            with v.Fori(0, RC // 2) as i:
                round1(i, True)
            with v.Fori(RC // 2, EARLY[0][0]) as i:
                round1(i, False)

            def rounds(first, stop, filled):
                if filled:
                    round1(first, False, True)
                with v.Fori(first + filled, stop) as i:
                    round1(i, False)

            def rest():
                onehots1(R1N * RG, 0, QT)
                onehots1(R1N * RG + 1, 1, 1)

            def to_nodes(first, *groups):
                v.wait_ge(y_r, RC)
                if first is not None:
                    v.wait_ge(agg1, first * RG + RG)
                    indices(first, 1)
                ranks_to_nodes(1, *groups)

            last_rounds(v, rounds, to_nodes, rest)

        @block.tensor
        def _(t):
            def offsets(n):
                _, values = nc.values_load_multi_w_load_instructions(
                    drow[0:1, bass.ds(n * QT + 1, QT - 1)], engines=(mybir.EngineType.PE,), min_val=0, max_val=WIN - P,
                    skip_runtime_bounds_check_because="a tile's first rank is at most 127 past that of the tile before")
                return [0, *values]

            def add_batch(bank, cols, rows, sl, offs):
                t.matmul(bank[0:cols, :], zrow[0:1, 0:cols], zrow[0:1, :], start=True, stop=False, skip_group_check=True)
                for j, r in enumerate(rows):
                    mm = t.matmul(bank[0:cols, bass.ds(offs[j], P)], r, U[:, sl, j, :], start=False,
                                  stop=(j == len(rows) - 1), skip_group_check=True)
                return mm

            t.wait_ge(consts, NCONST)
            t.wait_ge(falls, 1)
            for k in range(2):
                mm = t.matmul(B[0][0:1, 0:1], fall_q[:, k:k + 1], onesr[0:BT, 0:1], start=(k == 0), stop=(k == 1))
            mm.then_inc(falls_ps, 1)
            with if_unsorted(t):
                for placing in (False, True):
                    with t.Fori(0, NR) as n:
                        t.wait_ge(so_dve[placing], n * 11 + 2)
                        t.matmul(B[0][:, 0:P], onesr[:, :], eye_d, start=True, stop=True).then_inc(so_pe[placing], 1)
                    if not placing:
                        t.wait_ge(so_cntd, 1)
                        t.matmul(B[1][0:NP, 0:1], tri, upto[:, NJ - 1:NJ], start=True, stop=True).then_inc(so_cntp, 1)
            t.wait_ge(first_src, 1)
            t.transpose(B[1][:, 0:BT], srcf[:, :], ident[0:BT, 0:BT]).then_inc(first_p, 1)
            t.transpose(B[2][:, 0:BT], lof[:, :], ident[0:BT, 0:BT]).then_inc(first_p, 1)
            with t.Fori(0, NB) as b:
                t.wait_ge(pro, b * 5 + 1)
                t.transpose(B[0][:, 0:BT], srcf[:, :], ident[0:BT, 0:BT]).then_inc(pro_t, 1)
                t.wait_ge(pro, b * 5 + 2)
                t.transpose(B[1][:, 0:BT], relrow[:, :], ident[0:BT, 0:BT]).then_inc(pro_t, 1)
            t.wait_ge(pro, NB * 5)
            t.wait_ge(set_d, 3)
            t.transpose(B[0][0:NB, 0:BT], cnt[:, :], ident[0:BT, 0:BT]).then_inc(set_p, 1)
            t.transpose(B[0][0:NB, 128:128 + BT], st0[:, :], ident[0:BT, 0:BT]).then_inc(set_p, 1)
            t.wait_ge(set_d, 6)
            t.matmul(B[1][0:NB, 0:1], low[:, :], cum[:, BT - 1:BT], start=True, stop=True).then_inc(set_p, 1)
            t.wait_ge(ld_w, 7 * 16)
            t.matmul(B[2][:, 0:D], acol[:, 0:1].to_broadcast([D, P]), fcw[:, :], start=True, stop=True).then_inc(set_p, 1)
            t.matmul(B[2][:, 128:128 + D], acol[:, 1:2].to_broadcast([D, P]), fcw[:, :], start=True, stop=True).then_inc(set_p, 1)
            t.transpose(B[2][0:D, 256:256 + D], fcw[:, :], ident[0:D, 0:D]).then_inc(set_p, 1)
            t.wait_ge(set_d, 19)
            t.matmul(B[3][0:RC, 0:1], n_earlier, onesr[0:BT, 0:1], start=True, stop=True).then_inc(set_p, 1)

            t.wait_ge(acc_zero, 1)
            t.wait_ge(r0_ld, 32)
            def row_forms(b):
                t.wait_ge(prep, b * 11 + 7)
                t.transpose(LO_T, lof[:, :], ident[0:BT, 0:BT]).then_inc(prep_t, 1)
                t.transpose(ID_T, stdr[:, :], ident[0:BT, 0:BT]).then_inc(prep_t, 1)
                for k in range(3):
                    mm = t.matmul(ROWS[:, k, 0:BT], pack3[:, k:k + 1], ident[0:BT, 0:BT], start=True, stop=True)
                mm.then_inc(prep_t, 1)
                alone(t, prep, b * 11 + 10)

            def spread_hi(b, i, sl):
                t.wait_ge(hb_used, b * BB + i + 1)
                for j in range(QT):
                    mm = t.matmul(HBb[sl][0:NHI, j * P:(j + 1) * P],
                                  identb[0:BT, bass.ds(i * QT + j, 1)].to_broadcast([BT, NHI]),
                                  hib[:, :], start=True, stop=True)
                mm.then_inc(hb_ready, 1)

            def choose_hi(b, i, sl):
                n = b * BB + i
                t.wait_ge(onehot_hi, n + 3)
                t.wait_ge(ed_free, n + 1)
                for j in range(QT):
                    for c in range(3):
                        mm = t.matmul(EDb[sl][:, j, :], OH[:, sl, j * P:(j + 1) * P], EDp[:, c, :],
                                      start=(c == 0), stop=(c == 2))
                mm.then_inc(ed_ready, 1)

            def sum_batch(b, i, sl):
                n = b * BB + i
                offs = offsets(n)
                t.wait_ge(onehots, n + 1)
                t.wait_ge(mp_free, n + 1)
                add_batch(MPb[sl], C0, [SR[:, sl, j, :] for j in range(QT)], sl, offs).then_inc(agg, 1)

            def maxima(b):
                t.wait_ge(sm, b * 15 + 2)
                t.transpose(S_T, S[:, :], ident[:, :]).then_inc(sm_t, 1)
                t.wait_ge(sm, b * 15 + 3)
                t.matmul(TAILR, F1[:, P - 1:P], ident[0:BT, 0:BT], start=True, stop=True).then_inc(sm_t, 1)
                t.wait_ge(sm, b * 15 + 4)
                t.matmul(HEADR, Bh[:, 0:1], ident[0:BT, 0:BT], start=True, stop=True).then_inc(sm_t, 1)
                t.wait_ge(sm, b * 15 + 5)
                t.matmul(CINC, rowC[0:1, 0:BT], onesr[0:1, 0:1], start=True, stop=True).then_inc(sm_t, 1)
                t.wait_ge(sm, b * 15 + 7)
                t.matmul(CINK, rowK[0:1, :], onesr[0:1, 0:1], start=True, stop=True).then_inc(sm_t, 1)
                t.wait_ge(sm, b * 15 + 13)
                t.transpose(W_T, wr[:, :], ident[0:BT, 0:BT]).then_inc(sm_t, 1)
                t.wait_ge(sm, b * 15 + 14)
                t.matmul(FB, onesr[0:1, 0:C0], fr[0:1, 0:1], start=True, stop=True).then_inc(sm_t, 1)
                alone(t, exp_ready, b * 2 + 2)

            row_forms(0)
            spread_hi(0, 0, 0)
            with t.Fori(0, BB // 2 - 1) as i:
                for sl in range(2):
                    spread_hi(0, i * 2 + sl + 1, 1 - sl)
                    choose_hi(0, i * 2 + sl, sl)
            spread_hi(0, BB - 1, 1)
            choose_hi(0, BB - 2, 0)
            choose_hi(0, BB - 1, 1)
            maxima(0)
            with t.Fori(0, NB - 1) as b:
                row_forms(b + 1)
                spread_hi(b + 1, 0, 0)
                with t.Fori(0, BB // 2 - 1) as i:
                    for sl in range(2):
                        spread_hi(b + 1, i * 2 + sl + 1, 1 - sl)
                        sum_batch(b, i * 2 + sl, sl)
                        choose_hi(b + 1, i * 2 + sl, sl)
                spread_hi(b + 1, BB - 1, 1)
                for i in (BB - 2, BB - 1):
                    sum_batch(b, i, i % 2)
                    choose_hi(b + 1, i, i % 2)
                maxima(b + 1)
            with t.Fori(0, BB // 2 - 1) as i:
                for sl in range(2):
                    sum_batch(NB - 1, i * 2 + sl, sl)

            def rank_rows(L, g, k):
                cols, table, bank = (C0, R0, HP[k]) if L == 0 else (C1, R1, HQ[k])
                t.wait_ge(staged[L], g + 1)
                t.wait_ge(rows_r[L], g + 1)
                for j in range(CG):
                    mm = t.matmul(bank[:, j, :], accS[k][0:cols, j * P:(j + 1) * P], table[:, :], start=True, stop=True)
                mm.then_inc(rk_p[L], 1)

            def node_rows(L, g, k):
                t.wait_ge(rows_r[L], g + 3)
                t.wait_ge(centred[L], g * 3 + 1)
                for j in range(CG):
                    mm = t.matmul(HN[k][:, j, :], oh_n[k][:, j, :], rows_n[k][:, j, :], start=True, stop=True)
                mm.then_inc(node_p[L], 1)

            in_turn(t, ((rank_rows, 0), (node_rows, 1)), 0)

            def batch1(n, i, s, tiles):
                offs = offsets(n)
                t.wait_ge(u1, n + 1)
                t.wait_ge(g1[s], i * QT * 16 + tiles * 16)
                t.wait_ge(at1[s // HG], (i + 1) * 16)
                t.wait_ge(mp1_free, n + 1)
                add_batch(MPb[s % NS], C1, [ring[:, s * QT + j, :] for j in range(tiles)], s % NS, offs).then_inc(agg1, 1)

            def round1(i, self_term):
                for s in range(RG):
                    n = i * RG + s
                    h, q = s // HG, s % HG
                    if self_term and q == 1:
                        alone(t, xs_r, i * 2 + h + 1)
                        t.transpose(B[0][0:D, 0:P], xs[:, :], ident[:, :]).then_inc(xst_r, 1)
                    if self_term and q == 3:
                        t.wait_ge(xT_r, i * 2 + h + 1)
                        t.matmul(B[1][:, 0:D], xT[:, :], SW[:, :], start=True, stop=True).then_inc(y_p, 1)
                    batch1(n, i, s, QT)

            t.wait_ge(sw_ready, 1)
            t.wait_ge(ring_ones, 1)
            with t.Fori(0, RC // 2) as i:
                round1(i, True)
            with t.Fori(RC // 2, EARLY[0][0]) as i:
                round1(i, False)

            def rounds(first, stop, _):
                with t.Fori(first, stop) as i:
                    round1(i, False)

            def rest():
                batch1(R1N * RG, R1N, 0, QT)
                batch1(R1N * RG + 1, R1N, 1, 1)

            last_rounds(t, rounds, lambda _, *groups: in_turn(t, ((rank_rows, 0), (node_rows, 1)), 1, *groups), rest)

        @block.scalar
        def _(a):
            a.wait_ge(r0_ld, 32)
            a.wait_ge(acc_zero, 1)

            def first_rank(n):
                _, (r,) = nc.values_load_multi_w_load_instructions(
                    r0row[0:1, bass.ds(n, 1)], engines=(mybir.EngineType.Activation,), min_val=0, max_val=ACCW - WIN,
                    skip_runtime_bounds_check_because="there are at most N ranks, and one for each empty tile")
                return r

            def evacuate(bank, cols, n, free):
                r = first_rank(n)
                alone(a, agg if cols == C0 else agg1, n + 1 + (2 if cols == C0 else RG))
                alone(a, free, n + (2 if cols == C0 else NS))
                a.activation(acc[0:cols, bass.ds(r + 1, WIN - 1)], bank[0:cols, 1:WIN], ACT.Copy)
                a.activation(acc[0:cols, bass.ds(r, 1)], bank[0:cols, 0:1], ACT.Identity,
                             bias=acc[0:cols, bass.ds(r, 1)]).then_inc(free, 1)

            def onehot_of_hi(b, i, sl):
                n = b * BB + i
                a.wait_ge(hb_ready, n + 1)
                a.wait_ge(onehot_hi, n + 1)
                a.activation(HY[:, sl, :], HBb[sl][0:NHI, :], ACT.Abs, bias=nhi[0:NHI, 0:1]).then_inc(hb_used, 1)
                a.wait_ge(hb_used, n + 3)
                a.wait_ge(ed_ready, n + 1)
                a.activation(OH[:, sl, :], HY[:, sl, :], ACT.Relu, scale=-1.0, bias=onesr[0:NHI, 0:1]).then_inc(onehot_hi, 1)

            def weights(b):
                r = first_rank(b * BB)
                a.wait_ge(sm_t, b * 7 + 6)
                alone(a, sm, b * 15 + 15)
                a.activation(WD[:, :, 0], W_T, ACT.Exp).then_inc(exp_ready, 1)
                a.wait_ge(sm_t, b * 7 + 7)
                a.activation(Fs[:, :], FB, ACT.Exp, scale=fscale[:, 0:1]).then_inc(exp_ready, 1)
                alone(a, exp_ready, b * 2 + 2)
                alone(a, mp_free, b * BB + 2)
                a.activation(acc[0:C0, bass.ds(r, 1)], acc[0:C0, bass.ds(r, 1)], ACT.Identity,
                             scale=Fs[:, 0:1]).then_inc(rescaled, 1)
                alone(a, rescaled, b + 1)

            with a.Fori(0, BB // 2) as i:
                for sl in range(2):
                    onehot_of_hi(0, i * 2 + sl, sl)
            weights(0)
            with a.Fori(0, NB - 1) as b:
                with a.Fori(0, BB // 2) as i:
                    for sl in range(2):
                        onehot_of_hi(b + 1, i * 2 + sl, sl)
                        evacuate(MPb[sl], C0, b * BB + i * 2 + sl, mp_free)
                weights(b + 1)
            with a.Fori(0, BB // 2 - 1) as i:
                for sl in range(2):
                    evacuate(MPb[sl], C0, (NB - 1) * BB + i * 2 + sl, mp_free)
            a.wait_ge(mp_free, NB * BB - 2 + 2)
            a.wait_ge(rk_ld, 16)

            def stage_windows(L, g, k):
                cols = C0 if L == 0 else C1
                _, ranks = nc.values_load_multi_w_load_instructions(
                    rkrow[0:1, bass.ds(g * CG, CG)], engines=(mybir.EngineType.Activation,), min_val=0, max_val=ACCW - P,
                    skip_runtime_bounds_check_because="there are at most N ranks")
                a.wait_ge(rk_p[L], g + 1)
                for j in range(CG):
                    w = a.activation(accS[k][0:cols, j * P:(j + 1) * P], acc[0:cols, bass.ds(ranks[j], P)], ACT.Copy)
                w.then_inc(staged[L], 1)

            def square(L, g, k):
                a.wait_ge(centred[L], g * 3 + 9)
                a.activation(sqv[k], xv[:, bass.ds(g * CG, CG), :], ACT.Square).then_inc(squared[L], 1)

            def deviation(L, g, k):
                a.wait_ge(var_r[L], g + 1)
                a.activation(sd[:, k, :], var[:, k, :], ACT.Sqrt, scale=1.0 / D, bias=eps[:, 0:1]).then_inc(sd_r[L], 1)

            def ranks_to_nodes(L, *groups):
                in_turn(a, ((stage_windows, 0), (square, 2), (deviation, 3)), L, *groups)

            ranks_to_nodes(0)
            a.wait_ge(acc_zero1, 1)

            def round1(i, self_term):
                for s in range(RG):
                    if self_term and s % HG == 0:
                        a.activation(xs[:, :], xv[:, i * 2 + s // HG, :], ACT.Copy).then_inc(xs_r, 1)
                    evacuate(MPb[s % NS], C1, i * RG + s, mp1_free)

            with a.Fori(0, RC // 2) as i:
                round1(i, True)
            with a.Fori(RC // 2, EARLY[0][0]) as i:
                round1(i, False)

            def rounds(first, stop, _):
                with a.Fori(first, stop) as i:
                    round1(i, False)

            def rest():
                evacuate(MPb[0], C1, R1N * RG, mp1_free)
                evacuate(MPb[1], C1, R1N * RG + 1, mp1_free)

            def to_nodes(first, *groups):
                a.wait_ge(mp1_free, (R1N * RG + 2 if first is None else first * RG) + NS)
                ranks_to_nodes(1, *groups)

            last_rounds(a, rounds, to_nodes, rest)


_INS = ['x', 'src', 'dst', 'edge_attr_32', 'L0_gnn_fc_w', 'L0_gnn_attn_w', 'L1_gnn_msg_w', 'L1_gnn_msg_b',
        'L1_gnn_self_w', 'L1_gnn_self_b']


def kernel(**inputs):
    import numpy as _np
    import concourse.bacc as _bacc
    from concourse import mybir as _mybir
    from concourse.bass_utils import run_bass_kernel_spmd as _run

    nc = _bacc.Bacc("TRN2", target_bir_lowering=False, num_devices=1)
    arrays, args = {}, []
    for name in _INS:
        a = _np.ascontiguousarray(inputs[name])
        arrays[f"in_{name}_dram"] = a
        args.append(nc.dram_tensor(f"in_{name}_dram", a.shape, _mybir.dt.from_np(a.dtype), kind="ExternalInput").ap())
    args.append(nc.dram_tensor("out_0_dram", inputs['x'].shape, _mybir.dt.float32, kind="ExternalOutput").ap())
    gnn_layers(nc, *args)
    r = _run(nc, [arrays], core_ids=[0])
    return r.results[0]["out_0_dram"]
```
